# Optimizing a Trainium2 kernel written in Bass

```python
import numpy as np
import jax
import jax.numpy as jnp

def _softmax(x, axis=-1):
    return jax.nn.softmax(x, axis=axis)

def _gelu(x):
    return jax.nn.gelu(x, approximate=True)

def _silu(x):
    return jax.nn.silu(x)

def _sigmoid(x):
    return jax.nn.sigmoid(x)

def _layernorm(x, axis=-1, eps=1e-05):
    m = jnp.mean(x, axis=axis, keepdims=True)
    v = jnp.var(x, axis=axis, keepdims=True)
    return (x - m) / jnp.sqrt(v + eps)

def _scatter_add(tgt, idx, src, axis=0):
    return tgt.at[idx].add(src)

def _segment_sum(src, seg, n):
    return jax.ops.segment_sum(src, seg, n)
kernel_name = 'mk_xattn_seq_d2_seqx_r4_21ef65'

def setup_inputs(seed: int=0):
    np.random.seed(seed)
    _w = jnp.asarray

    def _rec_inputs():
        import jax
        import jax.numpy as jnp
        _rk = jax.random.key(seed)
        x = -0.000719 + 1.001 * jax.random.normal(jax.random.fold_in(_rk, 1), (4, 512, 320), jnp.float32)
        _lenS = 512 - jax.random.randint(jax.random.fold_in(_rk, 7), (4,), 0, max(1, 512 // 4) + 1, jnp.int32)
        _lenS2 = 1024 - jax.random.randint(jax.random.fold_in(_rk, 8), (4,), 0, max(1, 1024 // 4) + 1, jnp.int32)
        _ctx_2048P = jax.random.normal(jax.random.fold_in(_rk, 11), (4, 16, 512), jnp.float32)
        _ctx_2048c = jax.random.dirichlet(jax.random.fold_in(_rk, 511), 0.3 * jnp.ones((16,), jnp.float32), (4, 1024))
        _ctx_2048t = jnp.einsum('bsk,bkd->bsd', _ctx_2048c, _ctx_2048P)
        _ctx_2048t = _ctx_2048t * jax.lax.rsqrt(jnp.mean(jnp.square(_ctx_2048t)) + 1e-12) * 0.953939
        ctx_2048 = 0.00257118 + 0.99863 * (_ctx_2048t + 0.3 * jax.random.normal(jax.random.fold_in(_rk, 611), (4, 1024, 512), jnp.float32))
        fside_S_0 = jax.random.uniform(jax.random.fold_in(_rk, 12), (512,), jnp.float32, 0.0, 0.999706)
        return (x, ctx_2048, fside_S_0)
    x, ctx_2048, fside_S_0 = _rec_inputs()

    def _L0_xattn_setup():
        import jax, jax.numpy as jnp
        import numpy as np
        HEADS = 20
        NUM_TOKENS = 4
        IP_SCALE = 1.0
        SEM_SCALE = 0.5
        RESCALE = 1.0
        EPS = 1e-12

        def _l2norm(x, axis=-1):
            n = jnp.sqrt(jnp.sum(x * x, axis=axis, keepdims=True))
            return x / jnp.maximum(n, EPS)
        key = jax.random.key(seed)
        ks = jax.random.split(key, 10)
        B, S, C = (2, 256, 320)
        T, E = (81, 512)
        inp = {'hidden_states': jax.random.normal(ks[0], (B, S, C), jnp.float32), 'encoder_hidden_states': jax.random.normal(ks[1], (B, T, E), jnp.float32), 'spatial_mask': jax.random.uniform(ks[2], (S,), jnp.float32), 'W_q': jax.random.normal(ks[3], (C, C), jnp.float32) * C ** (-0.5), 'W_k': jax.random.normal(ks[4], (E, C), jnp.float32) * E ** (-0.5), 'W_v': jax.random.normal(ks[5], (E, C), jnp.float32) * E ** (-0.5), 'W_k_ip': jax.random.normal(ks[6], (E, C), jnp.float32) * E ** (-0.5), 'W_v_ip': jax.random.normal(ks[7], (E, C), jnp.float32) * E ** (-0.5), 'W_out': jax.random.normal(ks[8], (C, C), jnp.float32) * C ** (-0.5), 'b_out': jnp.zeros((C,), jnp.float32)}
        return inp
    _L0_xattn_all = _L0_xattn_setup()
    _L0_xattn_in = {k: v for k, v in _L0_xattn_all.items() if k in ('W_q', 'W_k', 'W_v', 'W_k_ip', 'W_v_ip', 'W_out', 'b_out')}
    del _L0_xattn_all

    def _L1_xattn_setup():
        import jax, jax.numpy as jnp
        import numpy as np
        NUM_HEADS = 20
        TEXT_LEN = 77
        IP_SCALE = 1.0

        def _attend(q, k, v, sm_scale):
            scores = jnp.einsum('bhsd,bhld->bhsl', q, k) * sm_scale
            probs = jax.nn.softmax(scores, axis=-1)
            return jnp.einsum('bhsl,bhld->bhsd', probs, v)

        def _split_heads(x, h):
            b, s, c = x.shape
            return x.reshape(b, s, h, c // h).transpose(0, 2, 1, 3)

        def _merge_heads(x):
            b, h, s, d = x.shape
            return x.transpose(0, 2, 1, 3).reshape(b, s, h * d)
        key = jax.random.key(seed)
        ks = jax.random.split(key, 8)
        B, S, C, CC, L = (8, 1024, 320, 512, TEXT_LEN + 4)
        sd_q = 1.0 / np.sqrt(C)
        sd_kv = 1.0 / np.sqrt(CC)
        return {'hidden_states': jax.random.normal(ks[0], (B, S, C), jnp.float32), 'encoder_hidden_states': jax.random.normal(ks[1], (B, L, CC), jnp.float32), 'Wq': jax.random.normal(ks[2], (C, C), jnp.float32) * sd_q, 'Wk': jax.random.normal(ks[3], (C, CC), jnp.float32) * sd_kv, 'Wv': jax.random.normal(ks[4], (C, CC), jnp.float32) * sd_kv, 'Wk_ip': jax.random.normal(ks[5], (C, CC), jnp.float32) * sd_kv, 'Wv_ip': jax.random.normal(ks[6], (C, CC), jnp.float32) * sd_kv, 'Wo': jax.random.normal(ks[7], (C, C), jnp.float32) * sd_q, 'bo': jnp.zeros((C,), jnp.float32)}
    _L1_xattn_all = _L1_xattn_setup()
    _L1_xattn_in = {k: v for k, v in _L1_xattn_all.items() if k in ('Wq', 'Wk', 'Wv', 'Wk_ip', 'Wv_ip', 'Wo', 'bo')}
    del _L1_xattn_all
    return {'x': x, 'ctx_2048': ctx_2048, 'fside_S_0': fside_S_0, 'L0_xattn_W_q': _L0_xattn_in['W_q'], 'L0_xattn_W_k': _L0_xattn_in['W_k'], 'L0_xattn_W_v': _L0_xattn_in['W_v'], 'L0_xattn_W_k_ip': _L0_xattn_in['W_k_ip'], 'L0_xattn_W_v_ip': _L0_xattn_in['W_v_ip'], 'L0_xattn_W_out': _L0_xattn_in['W_out'], 'L0_xattn_b_out': _L0_xattn_in['b_out'], 'L1_xattn_Wq': _L1_xattn_in['Wq'], 'L1_xattn_Wk': _L1_xattn_in['Wk'], 'L1_xattn_Wv': _L1_xattn_in['Wv'], 'L1_xattn_Wk_ip': _L1_xattn_in['Wk_ip'], 'L1_xattn_Wv_ip': _L1_xattn_in['Wv_ip'], 'L1_xattn_Wo': _L1_xattn_in['Wo'], 'L1_xattn_bo': _L1_xattn_in['bo']}

def reference(x, ctx_2048, fside_S_0, L0_xattn_W_q, L0_xattn_W_k, L0_xattn_W_v, L0_xattn_W_k_ip, L0_xattn_W_v_ip, L0_xattn_W_out, L0_xattn_b_out, L1_xattn_Wq, L1_xattn_Wk, L1_xattn_Wv, L1_xattn_Wk_ip, L1_xattn_Wv_ip, L1_xattn_Wo, L1_xattn_bo):
    import jax
    import jax.numpy as jnp

    def _L0_xattn_ref(hidden_states, encoder_hidden_states, spatial_mask, W_q, W_k, W_v, W_k_ip, W_v_ip, W_out, b_out):
        import jax, jax.numpy as jnp
        import numpy as np
        HEADS = 20
        NUM_TOKENS = 4
        IP_SCALE = 1.0
        SEM_SCALE = 0.5
        RESCALE = 1.0
        EPS = 1e-12

        def _l2norm(x, axis=-1):
            n = jnp.sqrt(jnp.sum(x * x, axis=axis, keepdims=True))
            return x / jnp.maximum(n, EPS)
        B, S, C = hidden_states.shape
        H = HEADS
        Dh = C // H
        attn_scale = Dh ** (-0.5)
        residual = hidden_states
        text_ehs = encoder_hidden_states[:, :-NUM_TOKENS]
        ip_ehs = encoder_hidden_states[:, -NUM_TOKENS:]

        def heads(x):
            return x.reshape(B, -1, H, Dh).transpose(0, 2, 1, 3)
        q = heads(hidden_states @ W_q)
        k_t = heads(text_ehs @ W_k)
        v_t = heads(text_ehs @ W_v)
        scores_t = jnp.einsum('bhsd,bhtd->bhst', q, k_t) * attn_scale
        probs_t = jax.nn.softmax(scores_t, axis=-1)
        text_out = jnp.einsum('bhst,bhtd->bhsd', probs_t, v_t)
        text_out = text_out.transpose(0, 2, 1, 3).reshape(B, S, C)
        k_ip = heads(ip_ehs @ W_k_ip)
        v_ip = heads(ip_ehs @ W_v_ip)
        attn_scores = jnp.einsum('bhsd,bhnd->bhsn', q, k_ip) * attn_scale
        qsem = jnp.einsum('bhst,bte->bhse', probs_t, text_ehs)
        qsem = _l2norm(qsem)
        ip_n = _l2norm(ip_ehs)
        sem = jnp.einsum('bhse,bne->bhsn', qsem, ip_n)
        sem = jax.lax.stop_gradient(sem)
        fused = attn_scores + SEM_SCALE * sem
        probs_ip = jax.nn.softmax(fused, axis=-1)
        probs_ip = probs_ip * spatial_mask[None, None, :, None]
        ip_out = jnp.einsum('bhsn,bhnd->bhsd', probs_ip, v_ip)
        ip_out = ip_out.transpose(0, 2, 1, 3).reshape(B, S, C)
        out = text_out + IP_SCALE * ip_out
        out = out @ W_out + b_out
        out = out + residual
        return out / RESCALE

    def _L1_xattn_ref(hidden_states, encoder_hidden_states, Wq, Wk, Wv, Wk_ip, Wv_ip, Wo, bo):
        import jax, jax.numpy as jnp
        import numpy as np
        NUM_HEADS = 20
        TEXT_LEN = 77
        IP_SCALE = 1.0

        def _attend(q, k, v, sm_scale):
            scores = jnp.einsum('bhsd,bhld->bhsl', q, k) * sm_scale
            probs = jax.nn.softmax(scores, axis=-1)
            return jnp.einsum('bhsl,bhld->bhsd', probs, v)

        def _split_heads(x, h):
            b, s, c = x.shape
            return x.reshape(b, s, h, c // h).transpose(0, 2, 1, 3)

        def _merge_heads(x):
            b, h, s, d = x.shape
            return x.transpose(0, 2, 1, 3).reshape(b, s, h * d)
        residual = hidden_states
        B, S, C = hidden_states.shape
        H = NUM_HEADS
        D = C // H
        sm_scale = 1.0 / jnp.sqrt(jnp.asarray(D, hidden_states.dtype))
        text = encoder_hidden_states[:, :TEXT_LEN, :]
        ip = encoder_hidden_states[:, TEXT_LEN:, :]
        q = _split_heads(hidden_states @ Wq.T, H)
        k = _split_heads(text @ Wk.T, H)
        v = _split_heads(text @ Wv.T, H)
        out_text = _merge_heads(_attend(q, k, v, sm_scale))
        k_ip = _split_heads(ip @ Wk_ip.T, H)
        v_ip = _split_heads(ip @ Wv_ip.T, H)
        out_ip = _merge_heads(_attend(q, k_ip, v_ip, sm_scale))
        out = out_text + IP_SCALE * out_ip
        out = out @ Wo.T + bo
        return out + residual
    x = _L0_xattn_ref(x, ctx_2048, fside_S_0, L0_xattn_W_q, L0_xattn_W_k, L0_xattn_W_v, L0_xattn_W_k_ip, L0_xattn_W_v_ip, L0_xattn_W_out, L0_xattn_b_out)
    x = _L1_xattn_ref(x, ctx_2048, L1_xattn_Wq, L1_xattn_Wk, L1_xattn_Wv, L1_xattn_Wk_ip, L1_xattn_Wv_ip, L1_xattn_Wo, L1_xattn_bo)
    return x

_drawn_inputs = setup_inputs


def setup_inputs(seed=0):
    import zlib

    import numpy as np

    out = dict(_drawn_inputs(seed))
    spreads = {'L0_xattn_b_out': (0.0, 0.1), 'L1_xattn_bo': (0.0, 0.1)}
    factors = {}
    for name, (base, spread) in spreads.items():
        noise = np.random.default_rng([zlib.crc32(name.encode()), seed]).standard_normal(out[name].shape)
        drawn = base * np.exp(spread * noise) if base else spread * noise
        out[name] = jnp.asarray(drawn.astype(out[name].dtype))
    for name, factor in factors.items():
        out[name] = (out[name] * factor).astype(out[name].dtype)
    return out
```

```python
from collections import deque
from contextlib import ExitStack
from functools import partial

import concourse.bass as bass
from concourse import mybir

ALU = mybir.AluOpType
ACT = mybir.ActivationFunctionType
F32 = mybir.dt.float32
F32R = mybir.dt.float32r
BF16 = mybir.dt.bfloat16
AX_X = mybir.AxisListType.X

P = 128
HEADS = 20
GROUP = 2
RING = 4
LOOK_MAX = 2
LOOK_LOAD = 3
IP = 4
TEXT1 = 77
EPS = 1e-12
SEM_SCALE = 0.5
ORDER = [(0, 0), (0, 1), (1, 0), (0, 2), (1, 1), (0, 3), (1, 2), (1, 3)]
Q_PARTS = (0, 0, 0, 1, 1, 2)
K_PARTS = (0, 1, 2, 0, 1, 0)
VCOLS = 41
AHEAD = 2
P_SLOTS = AHEAD + 1


class Sem:

    def __init__(self, handle):
        self.handle, self.value = handle, 0

    def ticket(self, by):
        self.value += by
        return (self, self.value)


class Queues:

    def __init__(self):
        self.q = {name: [] for name in ("pe", "act", "dve", "pool", "sp")}
        self.seen = {name: {} for name in self.q}

    def put(self, engine, fn, waits=(), sig=None, by=1):
        seen = self.seen[engine]
        need = {}
        for w in waits:
            if w is not None and seen.get(w[0], 0) < w[1]:
                need[w[0]] = max(need.get(w[0], 0), w[1])
        for s, v in need.items():
            seen[s] = v
        self.q[engine].append((list(need.items()), fn, sig, by))
        return sig.ticket(by) if sig is not None else None

    def play(self, engine, e):
        for need, fn, sig, by in self.q[engine]:
            for s, v in need:
                e.wait_ge(s.handle, v)
            ins = fn()
            if sig is not None:
                ins.then_inc(sig.handle, by)


def cross_attention_pair(nc, a, out):
    D = a["xT"].shape[1]
    B, SQ = a["xT"].shape[0], a["xT"].shape[2]
    E, T = a["ctxT"].shape[1], a["ctxT"].shape[2]
    DH = D // HEADS
    SCALE = float(DH) ** -0.5
    NM = -(-D // P)
    NE = E // P
    NT = T // P
    ST = SQ // P
    HS = HEADS * ST
    TEXT0 = T - IP
    NG = HEADS // GROUP
    mw = [min(P, D - P * m) for m in range(NM)]
    units = len(ORDER)

    ctx = ExitStack()
    with ctx:
        def sb(name, shape, dt=F32):
            return ctx.enter_context(nc.sbuf_tensor(name, shape, dt))

        def bank(name):
            return ctx.enter_context(nc.psum_tensor(name, [P, 512], F32))

        def sem(name):
            return Sem(ctx.enter_context(nc.semaphore(name)))

        def scratch(name, shape, dt):
            return nc.dram_tensor(name, shape, dt, kind="Internal").ap()

        q_scr = scratch("q_scr", (2, 3, D, SQ), BF16)
        k_scr = scratch("k_scr", (2, 3, D, T), BF16)
        v_scr = scratch("v_scr", (2, NT + 1, P, HEADS * VCOLS), F32)
        x1_scr = scratch("x1_scr", (B, D, SQ), F32)

        ident = sb("ident", [P, P])
        ones = sb("ones", [P, P])
        ones_col = sb("ones_col", [P, 1])
        ip_rows = sb("ip_rows", [P, 1])
        head_block = sb("head_block", [HEADS * IP, D])
        row_const = sb("row_const", [6, 2, T], BF16)
        mask_s = sb("mask_s", [P, ST])
        bias = sb("bias", [P, 2, NM])
        w_o = [sb(f"w_o{l}", [P, NM, D]) for l in range(2)]
        w_q = sb("w_q", [P, NM, D])
        w_text = sb("w_text", [P, NE, D + IP])
        w_ip = sb("w_ip", [P, NE, D])
        x_in = sb("x_in", [P, NM, SQ])
        ctx_t = sb("ctx_t", [P, NE, T])
        tok_stage = sb("tok_stage", [P, 2, E])
        tok_hi = sb("tok_hi", [P, NT, E], F32R)
        tok_lo = sb("tok_lo", [P, NT, E], F32R)
        q_ring = sb("q_ring", [102, RING, GROUP, SQ], BF16)
        k_ring = sb("k_ring", [102, RING, GROUP, T], BF16)
        v_ring = sb("v_ring", [P, RING, NT + 1, GROUP * VCOLS], F32R)
        prob = sb("prob", [P, 2, SQ])
        prob_hi = sb("prob_hi", [P, P_SLOTS, SQ], F32R)
        prob_lo = sb("prob_lo", [P, P_SLOTS, SQ], F32R)
        squares = sb("squares", [P, 2, E], BF16)
        max_parts = sb("max_parts", [P, 2, GROUP, ST, 3])
        neg_max = sb("neg_max", [P, 2, 2, GROUP * ST])
        MR = GROUP * ST
        max_t = sb("max_t", [2 * MR, P])
        max_r = sb("max_r", [2 * MR, P])
        max_bf = sb("max_bf", [2 * MR, 2, 3, P], BF16)
        ip_scores = sb("ip_scores", [P, 2, ST, HEADS, IP])
        sum_sq = sb("sum_sq", [P, 2, ST, HEADS])
        out_rows = sb("out_rows", [P, SQ])
        heads_out = sb("heads_out", [P, ST, HEADS, 66])
        row_const_f = heads_out[0:6].rearrange("p s h v -> p (s h v)")[:, 0:2 * T].rearrange(
            "p (l t) -> p l t", l=2)
        part_f = sb("part_f", [P, 2, SQ])
        part_r = sb("part_r", [P, 2, SQ])
        part_bf = sb("part_bf", [P, 2, 3, SQ], BF16)
        v_f = sb("v_f", [P, 2, D + IP])
        v_stage = sb("v_stage", [P, 2, HEADS, VCOLS], F32R)
        ip_sq = sb("ip_sq", [P, NE, IP])
        ip_n = sb("ip_n", [P, 2, IP])
        ip_rep = sb("ip_rep", [P, NE, HEADS, IP])
        v_block = sb("v_block", [HEADS * IP, 2, D])
        attn = sb("attn", [P, ST, HEADS, DH])
        ctx_flat = ctx_t[:].rearrange("p c t -> p (c t)")
        carved = [0]

        def carve(n):
            carved[0] += n
            return ctx_flat[:, carved[0] - n:carved[0]]

        attn2 = carve(HS * DH)
        w4 = carve(HS * IP)
        fused = carve(HS * IP)
        probs_t = carve(SQ)[0:HEADS * IP, :]
        o_t = carve(NM * SQ).rearrange("p (m s) -> p m s", m=NM)
        small = sb("small", [P, 6, HS])
        x_res = sb("x_res", [P, 1, SQ])
        x_out = sb("x_out", [P, 1, SQ])

        acc = [bank(f"acc{i}") for i in range(4)]
        score = [bank(f"score{i}") for i in range(2)]
        av0 = bank("av0")
        bg = bank("bg")

        s_const = sem("s_const")
        s_mem = sem("s_mem")
        s_x = sem("s_x")
        s_ctx = sem("s_ctx")
        s_wq = sem("s_wq")
        s_w = sem("s_w")
        s_tok = [sem(f"s_tok{i}") for i in range(2)]
        s_ring = [sem(f"s_ring{i}") for i in range(RING)]
        s_rows = [sem(f"s_rows{i}") for i in range(RING)]
        s_scr = [sem(f"s_scr{i}") for i in range(2)]
        s_part = [sem(f"s_part{i}") for i in range(2)]
        s_vout = [sem(f"s_vout{i}") for i in range(2)]
        s_res = [sem(f"s_res{i}") for i in range(1)]
        s_xout = [sem(f"s_xout{i}") for i in range(1)]
        s_score = sem("s_score")
        s_exp = sem("s_exp")
        s_lo = sem("s_lo")
        s_lo_pool = sem("s_lo_pool")
        s_main = sem("s_main")
        s_acc = sem("s_acc")
        s_sq = sem("s_sq")
        s_av = sem("s_av")
        s_bg = sem("s_bg")
        s_dve = sem("s_dve")
        s_pool = sem("s_pool")
        s_act = sem("s_act")

        qs = Queues()
        put = qs.put

        def dve(fn, *waits):
            return put("dve", fn, waits, s_dve)

        def pool(fn, *waits):
            return put("pool", fn, waits, s_pool)

        def act(fn, *waits):
            return put("act", fn, waits, s_act)

        def dma(dst, src, s, *waits):
            return put("sp", partial(nc.sync.dma_start, dst, src), waits, s, 16)

        c1 = [dma(ident[:], a["ident"], s_const), dma(head_block[:], a["head_block"], s_const),
              dma(row_const_f, a["row_const"], s_const), dma(ip_rows[:], a["ip_rows"], s_const),
              dma(mask_s[:], a["mask"], s_const)]
        for layer in range(2):
            for m in range(NM):
                c1.append(dma(w_o[layer][0:mw[m], m, :], a[f"wo{layer}"][P * m:P * m + mw[m], :], s_const))
                c1.append(dma(bias[0:mw[m], layer, m:m + 1], a[f"b{layer}"][P * m:P * m + mw[m], :], s_const))
        t_const = c1[-1]
        t_row_const = dve(partial(nc.vector.tensor_copy, row_const[:], row_const_f), t_const)
        put("dve", partial(nc.vector.memset, ones[:], 1.0), (), s_mem)
        put("dve", partial(nc.vector.memset, ones_col[:], 1.0), (), s_mem)
        t_mem = put("dve", partial(nc.vector.memset, out_rows[:], 0.0), (), s_mem)

        bg_free = [None]

        def bg_mm(fns, *waits):
            for fn in fns[:-1]:
                put("pe", fn, (*waits, bg_free[0]))
            return put("pe", fns[-1], (*waits, bg_free[0]), s_bg)

        def bg_read(fn, *waits):
            bg_free[0] = dve(fn, *waits)
            return bg_free[0]

        state = {"ring_used": [None] * RING, "x1": [None] * B, "x_in": None, "ctx_t": None,
                 "w_q": None, "w": None, "part": 0, "vst": 0,
                 "part_out": [None, None], "v_out": [None, None],
                 "scr_read": [None, None], "scr_done": [None, None], "v_block": [None, None]}

        def project(u):
            layer, b = ORDER[u]
            par = u % 2
            tasks = []
            box = {}

            def loads():
                src = a["xT"][b] if layer == 0 else x1_scr[b]
                for m in range(NM):
                    box["x"] = dma(x_in[0:mw[m], m, :], src[P * m:P * m + mw[m], :], s_x,
                                   state["x_in"], *( [state["x1"][b]] if layer else []))
                    box["wq"] = dma(w_q[0:mw[m], m, :], a[f"wq{layer}"][P * m:P * m + mw[m], :], s_wq,
                                    state["w_q"])
                box["ctx"] = dma(ctx_t[:], a["ctxT"][b].rearrange("(c p) t -> p c t", p=P), s_ctx,
                                 state["ctx_t"])
                dma(w_text[:, :, 0:D], a[f"wk{layer}"].rearrange("(c p) n -> p c n", p=P), s_w, state["w"])
                box["wk"] = dma(w_ip[:], a[f"wkip{layer}"].rearrange("(c p) n -> p c n", p=P), s_w, state["w"])
            tasks.append(loads)

            def split3(w, n, dst):
                i = state["part"] % 2
                state["part"] += 1
                f, r, h = part_f[0:w, i, 0:n], part_r[0:w, i, 0:n], part_bf[0:w, i, :, 0:n]
                t = bg_read(partial(nc.vector.tensor_copy, f, bg[0:w, 0:n]), (s_bg, s_bg.value), state["part_out"][i])
                t = dve(partial(nc.vector.tensor_copy, h[:, 0, :], f), t)
                t = pool(partial(nc.gpsimd.tensor_tensor, r, f, h[:, 0, :], ALU.subtract), t)
                t = dve(partial(nc.vector.tensor_copy, h[:, 1, :], r), t)
                t = pool(partial(nc.gpsimd.tensor_tensor, h[:, 2, :], r, h[:, 1, :], ALU.subtract), t)
                state["part_out"][i] = put("sp", partial(nc.sync.dma_start, dst, h), (t, state["scr_read"][par]),
                                           s_part[i], 16)
                box.setdefault("stores", {})[i] = state["part_out"][i]

            def q_task(m):
                def go():
                    w = mw[m]
                    bg_mm([partial(nc.tensor.matmul, bg[0:w, 0:SQ], w_q[0:mw[k], k, P * m:P * m + w],
                                                   x_in[0:mw[k], k, :], start=(k == 0), stop=(k == NM - 1))
                           for k in range(NM)], box["x"], box["wq"])
                    state["x_in"] = state["w_q"] = (s_bg, s_bg.value)
                    split3(w, SQ, q_scr[par, :, P * m:P * m + w, :].rearrange("j p t -> p j t"))
                return go
            tasks += [q_task(m) for m in range(NM)]

            def k_task(m, half):
                def go():
                    w = mw[m]
                    t0 = half * 512
                    edge = (TEXT0 if layer == 0 else TEXT1) - t0
                    edge = max(0, min(512, edge))
                    fns = []
                    for wt, lo, hi in ((w_text, 0, edge), (w_ip, edge, 512)):
                        if layer == 1 or True:
                            for k in range(NE):
                                if hi > lo:
                                    fns.append(partial(nc.tensor.matmul, bg[0:w, lo:hi], wt[:, k, P * m:P * m + w], ctx_t[:, k, t0 + lo:t0 + hi],
                                        start=(k == 0), stop=(k == NE - 1)))
                    bg_mm(fns, box["ctx"], box["wk"])
                    state["w"] = state["ctx_t"] = (s_bg, s_bg.value)
                    split3(w, 512, k_scr[par, :, P * m:P * m + w, t0:t0 + 512].rearrange("j p t -> p j t"))
                return go
            tasks += [k_task(m, half) for m in range(NM) for half in range(T // 512)]

            def v_loads():
                dma(w_text[:, :, 0:D], a[f"wv{layer}"].rearrange("(c p) n -> p c n", p=P), s_w, state["w"])
                box["wv"] = dma(w_ip[:], a[f"wvip{layer}"].rearrange("(c p) n -> p c n", p=P), s_w, state["w"])
            tasks.append(v_loads)

            ip_cols = ctx_t[:, :, T - IP:T]

            def ip_norm():
                t = dve(partial(nc.vector.tensor_tensor, ip_sq[:], ip_cols, ip_cols, ALU.mult), box["ctx"])
                bg_mm([partial(nc.tensor.matmul, bg[:, 0:IP], ones[:], ip_sq[:, k, :],
                                               start=(k == 0), stop=(k == NE - 1)) for k in range(NE)], t, t_mem)
                t = bg_read(partial(nc.vector.tensor_copy, ip_n[:, 0, :], bg[:, 0:IP]), (s_bg, s_bg.value))
                t = act(partial(nc.scalar.activation, ip_n[:, 1, :], ip_n[:, 0, :], ACT.Sqrt), t)
                t = dve(partial(nc.vector.tensor_scalar, ip_n[:, 0, :], ip_n[:, 1, :], EPS, None, ALU.max), t)
                t = dve(partial(nc.vector.reciprocal, ip_n[:, 1, :], ip_n[:, 0, :]), t)
                box["ipn"] = dve(partial(nc.vector.tensor_tensor, w_text[:, :, D:D + IP], ip_cols, ip_n[:, 1:2, :].broadcast_to([P, NE, IP]), ALU.mult),
                    t, state["w"])

            def ip_values():
                t = dve(partial(nc.vector.tensor_copy, ip_rep[:], ip_cols.rearrange("p c (o n) -> p c o n", o=1).broadcast_to([P, NE, HEADS, IP])),
                    box["ctx"])
                bg_mm([partial(nc.tensor.matmul, bg[0:HEADS * IP, 0:D],
                                               ip_rep[:, k, :, :].rearrange("p h n -> p (h n)"), w_ip[:, k, :],
                                               start=(k == 0), stop=(k == NE - 1)) for k in range(NE)],
                      t, box["wv"])
                state["v_block"][par] = bg_read(partial(nc.vector.tensor_tensor, v_block[:, par, :], bg[0:HEADS * IP, 0:D], head_block[:], ALU.mult),
                    (s_bg, s_bg.value), t_const)
                state["w"] = state["ctx_t"] = (s_bg, s_bg.value)
            if layer == 0:
                tasks += [ip_norm, ip_values]

            def v_task(blk):
                def go():
                    text = layer == 0 or blk == NT
                    c = 0 if blk == NT else blk
                    w = TEXT1 if blk == NT else P
                    n = D + IP if layer == 0 else D
                    wt = w_text if text else w_ip
                    bg_mm([partial(nc.tensor.matmul, bg[0:w, 0:n], ctx_t[:, k, c * P:c * P + w], wt[:, k, 0:n],
                                                   start=(k == 0), stop=(k == NE - 1)) for k in range(NE)],
                          box["ctx"], box["wv"], box.get("ipn"))
                    state["w"] = state["ctx_t"] = (s_bg, s_bg.value)
                    i = state["vst"] % 2
                    state["vst"] += 1
                    f, st = v_f[0:w, i, :], v_stage[0:w, i, :, :]
                    vf = f[:, 0:D].rearrange("p (h d) -> p h d", d=DH)
                    stf = v_stage.bitcast(F32)[0:w, i, :, :]
                    free = state["v_out"][i]
                    one = ip_rows if layer == 1 and blk == 0 else ones_col
                    t = bg_read(partial(nc.vector.tensor_scalar, f[:, 0:n], bg[0:w, 0:n], one[0:w, 0:1], None, ALU.mult),
                                (s_bg, s_bg.value), free, t_const, t_mem)
                    t1 = dve(partial(nc.vector.tensor_copy, st[:, :, 0:DH], vf), t)
                    t2 = dve(partial(nc.vector.tensor_copy, st[:, :, 2 * DH:2 * DH + 1], one[0:w, 0:1].rearrange("p (a b) -> p a b", a=1).broadcast_to([w, HEADS, 1])), free)
                    t3 = pool(partial(nc.gpsimd.tensor_tensor, st[:, :, DH:2 * DH], vf, stf[:, :, 0:DH], ALU.subtract), t1)
                    cols = 2 * DH + 1
                    if layer == 0:
                        ctx_ip = f[:, D:D + IP].rearrange("p (a n) -> p a n", a=1).broadcast_to([w, HEADS, IP])
                        t2 = dve(partial(nc.vector.tensor_copy, st[:, :, cols:cols + IP], ctx_ip), t)
                        t2 = dve(partial(nc.vector.tensor_tensor, st[:, :, cols + IP:cols + 2 * IP], ctx_ip,
                                                           stf[:, :, cols:cols + IP], ALU.subtract), t2)
                        cols += 2 * IP
                    state["v_out"][i] = put("sp", partial(nc.sync.dma_start, v_scr[par, blk, 0:w, :].rearrange("p (h v) -> p h v", v=VCOLS)[:, :, 0:cols], stf[:, :, 0:cols]),
                        (t2, t3, state["scr_read"][par]), s_vout[i], 16)
                    state["scr_done"][par] = (*box["stores"].values(), *[x for x in state["v_out"] if x])
                return go
            tasks += [v_task(blk) for blk in range(NT if layer == 0 else NT + 1)]
            return tasks

        def load_group(g):
            u, gi = divmod(g, NG)
            layer, par, slot = ORDER[u][0], u % 2, g % RING
            h0 = gi * GROUP
            w = (state["ring_used"][slot], *state["scr_done"][par])
            for i in range(6):
                rows = slice(DH * i, DH * i + DH)
                dma(k_ring[rows, slot, :, :],
                    k_scr[par, K_PARTS[i], h0 * DH:(h0 + GROUP) * DH, :].rearrange("(h d) t -> d h t", d=DH),
                    s_ring[slot], *w)
                dma(q_ring[rows, slot, :, :],
                    q_scr[par, Q_PARTS[i], h0 * DH:(h0 + GROUP) * DH, :].rearrange("(h d) t -> d h t", d=DH),
                    s_ring[slot], *w)
            for j in range(GROUP):
                dma(k_ring[96:102, slot, j, :], row_const[:, layer, :], s_ring[slot], t_row_const, *w)
            cols = slice(h0 * VCOLS, (h0 + GROUP) * VCOLS)
            if layer == 0:
                t = dma(v_ring.bitcast(F32)[:, slot, 0:NT, :], v_scr[par, 0:NT, :, cols].rearrange("b p v -> p b v"),
                        s_ring[slot], *w)
            else:
                for j in range(GROUP):
                    c0 = (h0 + j) * VCOLS
                    dma(v_ring.bitcast(F32)[:, slot, 0:NT, j * VCOLS:j * VCOLS + 33],
                        v_scr[par, 0:NT, :, c0:c0 + 33].rearrange("b p v -> p b v"), s_ring[slot], *w)
                    t = dma(v_ring.bitcast(F32)[0:TEXT1, slot, NT, j * VCOLS:j * VCOLS + 33],
                            v_scr[par, NT, 0:TEXT1, c0:c0 + 33], s_ring[slot], *w)
            ring_ready[g] = t
            state["scr_read"][par] = t

        ring_ready = {}
        rows_ready = {}

        def maxima(g):
            u, gi = divmod(g, NG)
            layer, slot, gp = ORDER[u][0], g % RING, g % 2
            tasks = []
            last = {}

            def half_task(j, st, half):
                def go():
                    bg_mm([partial(nc.tensor.matmul, bg[:, :], q_ring[0:96, slot, j, st * P:(st + 1) * P],
                                              k_ring[0:96, slot, j, half * 512:(half + 1) * 512],
                                              start=True, stop=True)], ring_ready[g])
                    ready = (s_bg, s_bg.value)
                    mp = max_parts[:, gp, j, st, :]

                    def top(i, lo, hi):
                        return bg_read(partial(nc.vector.tensor_reduce, mp[:, i:i + 1], bg[:, lo:hi], AX_X, ALU.max), ready)
                    if layer == 0:
                        top(half, 0, 512 if half == 0 else 512 - IP)
                        if half == 1:
                            bg_read(partial(nc.vector.tensor_copy, ip_scores[:, u % 2, st, gi * GROUP + j, :],
                                                            bg[:, 512 - IP:512]), ready)
                    elif half == 0:
                        top(0, 0, TEXT1)
                        top(1, TEXT1, 512)
                    else:
                        top(2, 0, 512)
                    last["t"] = bg_free[0]
                return go
            tasks += [half_task(j, st, half) for j in range(GROUP) for st in range(ST) for half in range(2)]

            def rows_task():
                mp = max_parts[:, gp, :, :, :].rearrange("p j s k -> p (j s) k")
                if layer == 0:
                    t = dve(partial(nc.vector.tensor_reduce, neg_max[:, gp, 0, :], mp[:, :, 0:2], AX_X, ALU.max,
                                                      negate=True), last["t"])
                else:
                    dve(partial(nc.vector.tensor_scalar, neg_max[:, gp, 0, :], mp[:, :, 0], -1.0, None, ALU.mult), last["t"])
                    t = dve(partial(nc.vector.tensor_reduce, neg_max[:, gp, 1, :], mp[:, :, 1:3], AX_X, ALU.max,
                                                      negate=True), last["t"])
                n = MR * (layer + 1)
                bg_mm([partial(nc.tensor.transpose, bg[0:n, 0:P], neg_max[:, gp, 0:layer + 1, :].rearrange("p a b -> p (a b)"),
                                             ident[:])], t, t_const)
                bf = max_bf[0:n, gp, :, :]
                t = bg_read(partial(nc.vector.tensor_copy, max_t[0:n, :], bg[0:n, 0:P]), (s_bg, s_bg.value),
                            rows_ready.get(g - 2))
                t = dve(partial(nc.vector.tensor_copy, bf[:, 0, :], max_t[0:n, :]), t)
                t = dve(partial(nc.vector.tensor_tensor, max_r[0:n, :], max_t[0:n, :], bf[:, 0, :], ALU.subtract), t)
                t = dve(partial(nc.vector.tensor_copy, bf[:, 1, :], max_r[0:n, :]), t)
                t = dve(partial(nc.vector.tensor_tensor, bf[:, 2, :], max_r[0:n, :], bf[:, 1, :], ALU.subtract), t)
                for k in range(layer + 1):
                    for i in range(3):
                        row = 96 + 3 * k + i
                        r = dma(q_ring[row:row + 1, slot, :, :].rearrange("p j (s c) -> p (j s) c", c=P),
                                max_bf[MR * k:MR * k + MR, gp, i, :], s_rows[slot], t, ring_ready[g])
                rows_ready[g] = r
            tasks.append(rows_task)
            return tasks

        tok_ready = {}
        tok_free = [None] * NT
        tok_split = [None, None]
        tok_count = [0]

        def load_tokens(b, c):
            i = tok_count[0] % 2
            tok_count[0] += 1
            t = put("sp", partial(nc.sync.dma_start, tok_stage[:, i, :], a["ctx"][b, c * P:(c + 1) * P, :]),
                    (tok_split[i],), s_tok[i], 16)
            t1 = dve(partial(nc.vector.tensor_copy, tok_hi[:, c, :], tok_stage[:, i, :]), t, tok_free[c])
            t2 = pool(partial(nc.gpsimd.tensor_tensor, tok_lo[:, c, :], tok_stage[:, i, :],
                                                tok_hi.bitcast(F32)[:, c, :], ALU.subtract), t1)
            tok_split[i] = t2
            tok_ready[(b, c)] = t2

        heads_read = [None]

        def bc(v, n):
            return v.rearrange("p (x o) -> p x o", o=1).broadcast_to([P, HS, n])

        def close(u):
            layer, b = ORDER[u]
            par = u % 2
            tasks = []
            box = {}
            ho = heads_out[:, :, :, :].rearrange("p s h v -> p (s h) v")
            at = attn[:].rearrange("p s h d -> p (s h) d")
            at2 = attn2.rearrange("p (x d) -> p x d", d=DH)
            rs, rs2 = small[:, 0, :], small[:, 1, :]
            fu = fused.rearrange("p (x n) -> p x n", n=IP)
            w4v = w4.rearrange("p (x n) -> p x n", n=IP)

            def combine():
                done = (s_dve, s_dve.value)
                dve_free = state["ctx_t"]
                t = dve(partial(nc.vector.tensor_tensor, at, ho[:, :, 0:DH], ho[:, :, DH:2 * DH], ALU.add), done)
                t1 = dve(partial(nc.vector.reciprocal, rs, ho[:, :, 2 * DH]), done)
                if layer == 0:
                    heads_read[0] = dve(partial(nc.vector.tensor_tensor, w4v, ho[:, :, 33:33 + IP], ho[:, :, 33 + IP:33 + 2 * IP], ALU.add), done, dve_free)
                    box["rs"] = t1
                    box["attn"] = dve(partial(nc.vector.tensor_tensor, at, at, bc(rs, DH), ALU.mult), t, t1)
                else:
                    t2 = dve(partial(nc.vector.tensor_tensor, at2, ho[:, :, 33:33 + DH], ho[:, :, 33 + DH:33 + 2 * DH],
                                                       ALU.add), done, dve_free)
                    heads_read[0] = dve(partial(nc.vector.reciprocal, rs2, ho[:, :, 65]), done)
                    t = dve(partial(nc.vector.tensor_tensor, at, at, bc(rs, DH), ALU.mult), t, t1)
                    t2 = dve(partial(nc.vector.tensor_tensor, at2, at2, bc(rs2, DH), ALU.mult), t2, heads_read[0])
                    box["attn"] = dve(partial(nc.vector.tensor_tensor, at, at, at2, ALU.add), t, t2)
            tasks.append(combine)

            def fuse():
                nrm, n2 = small[:, 2, :], small[:, 3, :]
                t = act(partial(nc.scalar.activation, nrm, sum_sq[:, par, :, :].rearrange("p s h -> p (s h)"), ACT.Sqrt),
                        (s_sq, s_sq.value))
                t = dve(partial(nc.vector.tensor_tensor, nrm, nrm, rs, ALU.mult), t, box["rs"])
                t = dve(partial(nc.vector.tensor_scalar, nrm, nrm, EPS, None, ALU.max), t)
                t = dve(partial(nc.vector.reciprocal, n2, nrm), t)
                t = dve(partial(nc.vector.tensor_tensor, n2, n2, rs, ALU.mult), t)
                t = dve(partial(nc.vector.tensor_tensor, w4v, w4v, bc(n2, IP), ALU.mult), t)
                t = dve(partial(nc.vector.tensor_scalar, w4v, w4v, SEM_SCALE, None, ALU.mult), t)
                t = dve(partial(nc.vector.scalar_tensor_tensor, fu, ip_scores[:, par, :, :, :].rearrange("p s h n -> p (s h) n"), SCALE, w4v,
                    ALU.mult, ALU.add), t)
                t = dve(partial(nc.vector.tensor_reduce, nrm, fu, AX_X, ALU.max), t)
                t = dve(partial(nc.vector.tensor_tensor, fu, fu, bc(nrm, IP), ALU.subtract), t)
                t = act(partial(nc.scalar.activation, fused, fused, ACT.Exp), t)
                t = dve(partial(nc.vector.tensor_reduce, nrm, fu, AX_X, ALU.add), t)
                t = dve(partial(nc.vector.reciprocal, n2, nrm), t)
                n2s = n2.rearrange("p (s h) -> p s h", h=HEADS)
                t = dve(partial(nc.vector.tensor_tensor, n2s, n2s, mask_s[:].rearrange("p (s o) -> p s o", o=1).broadcast_to([P, ST, HEADS]), ALU.mult),
                    t, t_const)
                box["probs"] = dve(partial(nc.vector.tensor_tensor, fu, fu, bc(n2, IP), ALU.mult), t)

            def probs_rows():
                bg_mm([partial(nc.tensor.transpose, bg[0:HEADS * IP, st * P:(st + 1) * P],
                                                    fused[:, st * HEADS * IP:(st + 1) * HEADS * IP], ident[:])
                       for st in range(ST)], box["probs"], t_const)
                box["pt"] = bg_read(partial(nc.vector.tensor_copy, probs_t, bg[0:HEADS * IP, :]), (s_bg, s_bg.value))
            if layer == 0:
                tasks += [fuse, probs_rows]

            def turn(m):
                def go():
                    w = mw[m]
                    fl = [attn[:, st, :, :].rearrange("p h d -> p (h d)")[:, P * m:P * m + w] for st in range(ST)]
                    if layer == 0:
                        fns = [partial(nc.tensor.matmul, bg[0:w, :], v_block[:, par, P * m:P * m + w], probs_t,
                                                  start=True, stop=True)]
                        fns += [partial(nc.tensor.matmul, bg[0:w, st * P:(st + 1) * P], fl[st], ident[:],
                                                          start=False, stop=True, skip_group_check=True)
                                for st in range(ST)]
                        bg_mm(fns, box["attn"], box["pt"], state["v_block"][par], t_const)
                    else:
                        bg_mm([partial(nc.tensor.transpose, bg[0:w, st * P:(st + 1) * P], fl[st], ident[:])
                               for st in range(ST)], box["attn"], t_const)
                    box["o"] = bg_read(partial(nc.vector.tensor_copy, o_t[0:w, m, :], bg[0:w, :]), (s_bg, s_bg.value))
                return go
            tasks += [turn(m) for m in range(NM)]

            def finish(m):
                def go():
                    w, i = mw[m], (NM * u + m) % 1
                    src = a["xT"][b] if layer == 0 else x1_scr[b]
                    r = put("sp", partial(nc.sync.dma_start, x_res[0:w, i, :], src[P * m:P * m + w, :]),
                            (fin_free[i], state["x1"][b] if layer else None), s_res[i], 16)
                    bg_mm([partial(nc.tensor.matmul, bg[0:w, :], w_o[layer][0:mw[k], k, P * m:P * m + w],
                                                   o_t[0:mw[k], k, :], start=(k == 0), stop=(k == NM - 1))
                           for k in range(NM)], box["o"], t_const)
                    state["ctx_t"] = (s_bg, s_bg.value)
                    t = bg_read(partial(nc.vector.scalar_tensor_tensor, x_out[0:w, i, :], bg[0:w, :], bias[0:w, layer, m:m + 1], x_res[0:w, i, :],
                        ALU.add, ALU.add), (s_bg, s_bg.value), r, xout_free[i])
                    fin_free[i] = t
                    dst = (x1_scr if layer == 0 else out)[b, P * m:P * m + w, :]
                    xout_free[i] = put("sp", partial(nc.sync.dma_start, dst, x_out[0:w, i, :]), (t,), s_xout[i], 16)
                    if layer == 0:
                        state["x1"][b] = xout_free[i]
                        x1_stores.setdefault(b, {})[i] = xout_free[i]
                return go
            tasks += [finish(m) for m in range(NM)]
            return tasks

        fin_free, xout_free, x1_stores = [None], [None], {}

        chunks = [(u, h, c) for u in range(units) for h in range(HEADS) for c in range(NT)]
        exp_done = {}
        lo_done = {}
        main_done = {}
        acc_free = [[] for _ in range(4)]
        av_free = [None]
        rows_free = [None]

        def rows_of(u, c):
            return P - IP if ORDER[u][0] == 0 and c == NT - 1 else P

        def scores(n):
            u, h, c = chunks[n]
            layer = ORDER[u][0]
            g, j = u * NG + h // GROUP, h % GROUP
            slot, kk = g % RING, rows_of(u, c)
            depth = 96 + 3 * (layer + 1)
            bank_s, ps, es = score[n % 2], n % P_SLOTS, n % 2
            t = put("pe", partial(nc.tensor.matmul, bank_s[0:kk, :], k_ring[0:depth, slot, j, c * P:c * P + kk],
                                             q_ring[0:depth, slot, j, :], start=True, stop=True),
                    (ring_ready[g], rows_ready[g], exp_done.get(n - 2)), s_score)
            put("act", partial(nc.scalar.activation, prob[0:kk, es, :], bank_s[0:kk, :], ACT.Exp, scale=SCALE),
                (t, lo_done.get(n - 2)))
            exp_done[n] = put("act", partial(nc.scalar.activation, prob_hi[0:kk, ps, :], bank_s[0:kk, :], ACT.Exp,
                                                            scale=SCALE),
                              (t, main_done.get(n - P_SLOTS)), s_exp)

        def low_part(n):
            u, h, c = chunks[n]
            kk, ps, es = rows_of(u, c), n % P_SLOTS, n % 2
            on_pool = ORDER[u][0] == 1 and n % 3 == 0
            unit = nc.gpsimd if on_pool else nc.vector
            lo_done[n] = put("pool" if on_pool else "dve", partial(unit.tensor_tensor,
                prob_lo[0:kk, ps, :], prob[0:kk, es, :], prob_hi.bitcast(F32)[0:kk, ps, :], ALU.subtract),
                (exp_done[n], main_done.get(n - P_SLOTS)), s_lo_pool if on_pool else s_lo)

        def products0(n, slot_hook):
            u, h, c = chunks[n]
            g, j = u * NG + h // GROUP, h % GROUP
            slot, kk, ps = g % RING, rows_of(u, c), n % P_SLOTS
            b = ORDER[u][1]
            first, last = c == 0, c == NT - 1
            for st in range(ST):
                cols = slice(st * P, (st + 1) * P)
                w = [exp_done[n], tok_ready[(b, c)]] + (acc_free[st] if first else [])
                put("pe", partial(nc.tensor.matmul, acc[st][:, :], prob_hi[0:kk, ps, cols], tok_hi[0:kk, c, :],
                                             start=first, stop=False), w)
                put("pe", partial(nc.tensor.matmul, acc[st][:, :], prob_hi[0:kk, ps, cols], tok_lo[0:kk, c, :],
                                             start=False, stop=False))
                t = put("pe", partial(nc.tensor.matmul, acc[st][:, :], prob_lo[0:kk, ps, cols], tok_hi[0:kk, c, :],
                                                 start=False, stop=last), (lo_done[n],),
                        s_acc if last else None)
                if last:
                    ts = put("act", partial(nc.scalar.activation, squares[:, st % 2, :], acc[st][:, :], ACT.Square,
                        accum_out=sum_sq[:, u % 2, st, h:h + 1]), (t, (s_sq, s_sq.value - 1)), s_sq)
                    acc_free[st] = [ts]
                slot_hook()
            for i, pr in enumerate((prob_hi, prob_lo)):
                t = put("pe", partial(nc.tensor.matmul, av0[0:VCOLS, :], v_ring[0:kk, slot, c, j * VCOLS:(j + 1) * VCOLS], pr[0:kk, ps, :],
                    start=(first and i == 0), stop=(last and i == 1)), (av_free[0],),
                    s_main if i else None)
            main_done[n] = t
            tok_free[c] = t
            if last:
                t = put("act", partial(nc.scalar.activation, out_rows[0:VCOLS, :], av0[0:VCOLS, :], ACT.Copy),
                        (t, rows_free[0], t_mem), s_av)
                av_free[0] = t
                urgent.append(lambda: turn_head(u, h, t))

        def products1(n, slot_hook):
            u, h, c = chunks[n]
            g, j = u * NG + h // GROUP, h % GROUP
            slot, ps = g % RING, n % P_SLOTS
            first, last = c == 0, c == NT - 1
            bi = 2 * (h % 2)
            M = 2 * DH + 1
            vc = slice(j * VCOLS, j * VCOLS + M)
            for i, pr in enumerate((prob_hi, prob_lo)):
                w = [exp_done[n] if i == 0 else lo_done[n]] + (acc_free[bi] + acc_free[bi + 1] if first else [])
                if first:
                    put("pe", partial(nc.tensor.matmul, acc[bi + 1][0:M, :], v_ring[0:TEXT1, slot, NT, vc], pr[0:TEXT1, ps, :],
                        start=(i == 0), stop=(i == 1)), w)
                t = put("pe", partial(nc.tensor.matmul, acc[bi][0:M, :], v_ring[:, slot, c, vc], pr[:, ps, :],
                    start=(first and i == 0), stop=(last and i == 1)), w, s_main if i else None)
                slot_hook()
            main_done[n] = t
            if last:
                ta = put("act", partial(nc.scalar.activation, out_rows[0:M, :], acc[bi + 1][0:M, :], ACT.Copy),
                         (t, rows_free[0], t_mem), s_av)
                tb = put("act", partial(nc.scalar.activation, out_rows[64:64 + M, :], acc[bi][0:M, :], ACT.Copy),
                         (t, rows_free[0]), s_av)
                acc_free[bi], acc_free[bi + 1] = [tb], [ta]
                urgent.append(lambda: turn_head(u, h, tb))

        def turn_head(u, h, t):
            layer = ORDER[u][0]
            w = VCOLS if layer == 0 else 64 + 2 * DH + 1
            bg_mm([partial(nc.tensor.transpose, bg[:, st * P:st * P + w], out_rows[0:w, st * P:(st + 1) * P],
                                                ident[0:w, 0:w]) for st in range(ST)], t, t_const)
            rows_free[0] = (s_bg, s_bg.value)
            src = bg[:, :].rearrange("p (s v) -> p s v", v=P)
            if layer == 0:
                bg_read(partial(nc.vector.tensor_copy, heads_out[:, :, h, 0:VCOLS], src[:, :, 0:VCOLS]),
                        (s_bg, s_bg.value), heads_read[0])
            else:
                bg_read(partial(nc.vector.tensor_copy, heads_out[:, :, h, 0:33], src[:, :, 0:33]),
                        (s_bg, s_bg.value), heads_read[0])
                bg_read(partial(nc.vector.tensor_copy, heads_out[:, :, h, 33:66], src[:, :, 64:97]),
                        (s_bg, s_bg.value), heads_read[0])

        urgent = deque()

        for c in range(2):
            load_tokens(0, c)
        for t in project(0):
            t()
        for c in range(2, NT):
            load_tokens(0, c)
        groups = units * NG
        for g in range(LOOK_LOAD):
            load_group(g)
        for g in range(LOOK_MAX):
            for t in maxima(g):
                t()

        per_group = GROUP * NT
        for n in range(AHEAD):
            scores(n)
            low_part(n)
        l0_units = [u for u in range(units) if ORDER[u][0] == 0]
        bgq, unit_q = deque(), deque()
        for g in range(groups):
            u, gi = divmod(g, NG)
            if g + LOOK_LOAD < groups:
                load_group(g + LOOK_LOAD)
            if gi == 0:
                unit_q.clear()
                if u >= 1:
                    combine, *rest = close(u - 1)
                    urgent.append(combine)
                    unit_q.extend(rest)
                if u + 1 < units:
                    unit_q.extend(project(u + 1))
                per = -(-len(unit_q) // (NG - LOOK_LOAD))
            work = list(maxima(g + LOOK_MAX)) if g + LOOK_MAX < groups else []
            mine = [unit_q.popleft() for _ in range(min(per, len(unit_q)))]
            tasks = []
            for i in range(max(len(work), 1)):
                tasks += work[i:i + 1]
                lo, hi = len(mine) * i // max(len(work), 1), len(mine) * (i + 1) // max(len(work), 1)
                tasks += mine[lo:hi]
            bgq.extend(tasks)
            slots = per_group * (ST if ORDER[u][0] == 0 else 2)
            total, done = len(bgq), [0, 0]

            def hook():
                done[0] += 1
                if urgent:
                    urgent.popleft()()
                    return
                while bgq and done[1] < -(-total * done[0] // slots):
                    done[1] += 1
                    bgq.popleft()()

            for n in range(g * per_group, (g + 1) * per_group):
                if n + AHEAD < len(chunks):
                    scores(n + AHEAD)
                    low_part(n + AHEAD)
                (products0 if ORDER[u][0] == 0 else products1)(n, hook)
                _, h, c = chunks[n]
                if u in l0_units and h == HEADS - 1 and u != l0_units[-1]:
                    load_tokens(ORDER[l0_units[l0_units.index(u) + 1]][1], c)
            while bgq:
                bgq.popleft()()
            state["ring_used"][g % RING] = main_done[(g + 1) * per_group - 1]
        while urgent:
            urgent.popleft()()
        for t in close(units - 1):
            t()
        qs.q["sp"].append(([x for x in xout_free], None, None, 0))

        block = ctx.enter_context(nc.Block())

        @block.tensor
        def _(e):
            qs.play("pe", e)

        @block.scalar
        def _(e):
            qs.play("act", e)

        @block.vector
        def _(e):
            qs.play("dve", e)

        @block.gpsimd
        def _(e):
            qs.play("pool", e)

        @block.sync
        def _(e):
            final = qs.q["sp"].pop()
            qs.play("sp", e)
            for s, v in final[0]:
                e.wait_ge(s.handle, v)
            for s in (*s_part, *s_vout, *s_xout):
                e.wait_ge(s.handle, s.value)


def kernel(**inputs):
    import numpy as np
    import concourse.bacc as bacc
    from concourse.bass_utils import run_bass_kernel_spmd

    f = {k: np.asarray(v) for k, v in inputs.items()}
    x, c = f["x"], f["ctx_2048"]
    B, S, D = x.shape
    T = c.shape[1]
    tr = lambda v: np.ascontiguousarray(np.swapaxes(v, -1, -2))
    row_const = np.zeros((6, 2, T), np.float32)
    row_const[:, 0, :] = 1.0
    row_const[0:3, 1, :TEXT1] = 1.0
    row_const[3:6, 1, TEXT1:] = 1.0
    ip_rows = np.ones((P, 1), np.float32)
    ip_rows[:TEXT1] = 0.0
    arrays = {
        "xT": tr(x), "ctxT": tr(c), "ctx": np.ascontiguousarray(c),
        "mask": tr(f["fside_S_0"].reshape(S // P, P)),
        "ident": np.eye(P, dtype=np.float32), "row_const": row_const, "ip_rows": ip_rows,
        "head_block": np.kron(np.eye(HEADS, dtype=np.float32), np.ones((IP, D // HEADS), np.float32)),
    }
    for name, key in (("wq", "W_q"), ("wk", "W_k"), ("wv", "W_v"), ("wkip", "W_k_ip"), ("wvip", "W_v_ip"),
                      ("wo", "W_out")):
        arrays[name + "0"] = np.ascontiguousarray(f["L0_xattn_" + key])
    for name, key in (("wq", "Wq"), ("wk", "Wk"), ("wv", "Wv"), ("wkip", "Wk_ip"), ("wvip", "Wv_ip"), ("wo", "Wo")):
        arrays[name + "1"] = tr(f["L1_xattn_" + key])
    arrays["b0"] = f["L0_xattn_b_out"].reshape(D, 1)
    arrays["b1"] = f["L1_xattn_bo"].reshape(D, 1)

    nc = bacc.Bacc("TRN2", target_bir_lowering=False, num_devices=1)
    aps = {k: nc.dram_tensor(f"in_{k}", v.shape, F32, kind="ExternalInput").ap() for k, v in arrays.items()}
    out = nc.dram_tensor("out_T", (B, D, S), F32, kind="ExternalOutput").ap()
    cross_attention_pair(nc, aps, out)
    r = run_bass_kernel_spmd(nc, [{f"in_{k}": v for k, v in arrays.items()}], core_ids=[0])
    return tr(r.results[0]["out_T"])
```

```python
import math
from collections import deque
from contextlib import ExitStack
from functools import partial

import concourse.bass as bass
from concourse import mybir

ALU = mybir.AluOpType
ACT = mybir.ActivationFunctionType
F32 = mybir.dt.float32
F32R = mybir.dt.float32r
BF16 = mybir.dt.bfloat16
AX_X = mybir.AxisListType.X

P = 128
HEADS = 20
GROUP = 2
RING = 4
LOOK_MAX = 2
LOOK_LOAD = 3
IP = 4
TEXT1 = 77
EPS = 1e-12
SEM_SCALE = 0.5
LAYER_LAG = 17
WEIGHT = (4, 1)
Q_PARTS = (0, 0, 0, 1, 1, 2)
K_PARTS = (0, 1, 2, 0, 1, 0)
VCOLS = 41
CTX_COL = 16
SUM_COL = (20, 32)
AHEAD = 3
P_SLOTS = AHEAD + 1
POOL_LOW = (0, 2, 3, 5, 6)
LOW_LAG = 1
E_SLOTS = 4
SPACING = 2


class Sem:

    def __init__(self, handle):
        self.handle, self.value = handle, 0

    def ticket(self, by):
        self.value += by
        return (self, self.value)


class Bank:

    def __init__(self, tensor):
        self.tensor, self.free = tensor, []

    def __getitem__(self, key):
        return self.tensor[key]


class Queues:

    def __init__(self):
        self.q = {name: [] for name in ("pe", "act", "dve", "pool", "sp")}
        self.seen = {name: {} for name in self.q}

    def put(self, engine, fn, waits=(), sig=None, by=1):
        seen = self.seen[engine]
        need = {}
        for w in waits:
            if w is not None and seen.get(w[0], 0) < w[1]:
                need[w[0]] = max(need.get(w[0], 0), w[1])
        for s, v in need.items():
            seen[s] = v
        self.q[engine].append((list(need.items()), fn, sig, by))
        return sig.ticket(by) if sig is not None else None

    def play(self, engine, e):
        for need, fn, sig, by in self.q[engine]:
            for s, v in need:
                e.wait_ge(s.handle, v)
            ins = fn()
            if sig is not None:
                ins.then_inc(sig.handle, by)


def cross_attention_pair(nc, a, out):
    D = a["xT"].shape[1]
    B, SQ = a["xT"].shape[0], a["xT"].shape[2]
    E, T = a["ctxT"].shape[1], a["ctxT"].shape[2]
    DH = D // HEADS
    SCALE = float(DH) ** -0.5
    NM = -(-D // P)
    NE = E // P
    NT = T // P
    ST = SQ // P
    HS = HEADS * ST
    TEXT0 = T - IP
    NG = HEADS // GROUP
    mw = [min(P, D - P * m) for m in range(NM)]
    units = [(layer, b) for layer in range(2) for b in range(B)]
    seq = []
    for k in range(B * NG + LAYER_LAG):
        if k < B * NG:
            seq.append((k // NG, k % NG))
        if k >= LAYER_LAG:
            seq.append((B + (k - LAYER_LAG) // NG, (k - LAYER_LAG) % NG))
    place = {x: i for i, x in enumerate(seq)}

    ctx = ExitStack()
    with ctx:
        def sb(name, shape, dt=F32):
            return ctx.enter_context(nc.sbuf_tensor(name, shape, dt))

        def bank(name):
            return Bank(ctx.enter_context(nc.psum_tensor(name, [P, 512], F32)))

        def sem(name):
            return Sem(ctx.enter_context(nc.semaphore(name)))

        def scratch(name, shape, dt):
            return nc.dram_tensor(name, shape, dt, kind="Internal").ap()

        q_scr = scratch("q_scr", (2 * B, 3, D, SQ), BF16)
        k_scr = scratch("k_scr", (2 * B, 3, D, T), BF16)
        v_scr = scratch("v_scr", (2 * B, NT + 1, P, HEADS * VCOLS), F32)
        row_scr = scratch("row_scr", (6, 2, T), BF16)
        x1_scr = scratch("x1_scr", (B, D, SQ), F32)

        ident = sb("ident", [P, P])
        ones = sb("ones", [P, P])
        ones_col = sb("ones_col", [P, 1])
        ip_rows = sb("ip_rows", [P, 1])
        head_block = sb("head_block", [HEADS * IP, D])
        mask_s = sb("mask_s", [P, ST])
        bias = sb("bias", [P, 2, NM])
        w_o = [sb(f"w_o{l}", [P, NM, D]) for l in range(2)]
        w_q = sb("w_q", [P, NM, D])
        w_text = sb("w_text", [P, NE, D + IP])
        w_ip = sb("w_ip", [P, NE, D])
        x_in = sb("x_in", [P, NM, SQ])
        ctx_t = sb("ctx_t", [P, NE, T])
        tok_stage = sb("tok_stage", [P, 2, E])
        tok_hi = sb("tok_hi", [P, NT, E], F32R)
        tok_lo = sb("tok_lo", [P, NT, E], F32R)
        q_ring = sb("q_ring", [102, RING, GROUP, SQ], BF16)
        k_ring = sb("k_ring", [102, RING, GROUP, T], BF16)
        v_ring = sb("v_ring", [P, RING, NT + 1, GROUP * VCOLS], F32R)
        prob = sb("prob", [P, E_SLOTS, SQ])
        prob_hi = sb("prob_hi", [P, P_SLOTS, SQ], F32R)
        prob_lo = sb("prob_lo", [P, P_SLOTS, SQ], F32R)
        squares = sb("squares", [P, 2, E], BF16)
        max_parts = sb("max_parts", [P, 2, GROUP, ST, 3])
        neg_max = sb("neg_max", [P, 2, 2, GROUP * ST])
        MR = GROUP * ST
        max_t = sb("max_t", [2 * MR, P])
        max_r = sb("max_r", [2 * MR, P])
        max_bf = sb("max_bf", [2 * MR, 2, 3, P], BF16)
        ip_scores = sb("ip_scores", [P, 2, ST, HEADS, IP])
        sum_sq = sb("sum_sq", [P, 2, ST, HEADS])
        out_rows = sb("out_rows", [P, 2, SQ])
        heads_out = [sb(f"heads_out{l}", [P, ST, HEADS, n]) for l, n in enumerate((DH + IP + 1, 2 * DH + 2))]
        row_const_f = heads_out[1][0:6].rearrange("p s h v -> p (s h v)")[:, 0:2 * T].rearrange(
            "p (l t) -> p l t", l=2)
        first_v_text = heads_out[0].rearrange("p s h v -> p (s h v)")[:, 0:NE * (D + IP)].rearrange(
            "p (c n) -> p c n", c=NE)
        part_f = sb("part_f", [P, 2, SQ])
        part_r = sb("part_r", [P, 2, SQ])
        part_bf = sb("part_bf", [P, 2, 3, SQ], BF16)
        v_f = sb("v_f", [P, 2, D + IP])
        v_stage = sb("v_stage", [P, 2, HEADS, VCOLS], F32R)
        ip_sq = sb("ip_sq", [P, NE, IP])
        ip_n = sb("ip_n", [P, 2, IP])
        ip_rep = sb("ip_rep", [P, NE, HEADS, IP])
        v_block = sb("v_block", [HEADS * IP, 2, D])
        attn = sb("attn", [P, ST, HEADS, DH])
        first_v_ip = attn[:].rearrange("p s h d -> p (s h d)")[:, 0:NE * D].rearrange("p (c n) -> p c n", c=NE)
        w4 = sb("w4", [P, HS * IP])
        ctx_flat = ctx_t[:].rearrange("p c t -> p (c t)")
        carved = [0]

        def carve(n):
            carved[0] += n
            return ctx_flat[:, carved[0] - n:carved[0]]

        fused = carve(HS * IP)
        probs_t = carve(SQ)[0:HEADS * IP, :]
        o_t = carve(NM * SQ).rearrange("p (m s) -> p m s", m=NM)
        small = sb("small", [P, 6, HS])
        x_res, x_out = part_r, part_f

        acc = [bank(f"acc{i}") for i in range(4)]
        score = [bank(f"score{i}") for i in range(2)]
        av0 = bank("av0")
        spare = bank("spare")

        s_const = sem("s_const")
        s_mem = sem("s_mem")
        s_rowf = sem("s_rowf")
        s_rowc = sem("s_rowc")
        s_wo = sem("s_wo")
        s_wv0 = sem("s_wv0")
        s_x = sem("s_x")
        s_ctx = sem("s_ctx")
        s_wq = sem("s_wq")
        s_w = sem("s_w")
        s_tok = [sem(f"s_tok{i}") for i in range(2)]
        s_ring = [sem(f"s_ring{i}") for i in range(RING)]
        s_ring_v = [sem(f"s_ring_v{i}") for i in range(RING)]
        s_rows = [sem(f"s_rows{i}") for i in range(RING)]
        s_scr = [sem(f"s_scr{i}") for i in range(2)]
        s_part = [sem(f"s_part{i}") for i in range(2)]
        s_vout = [sem(f"s_vout{i}") for i in range(2)]
        s_res = [sem(f"s_res{i}") for i in range(2)]
        s_xout = [sem(f"s_xout{i}") for i in range(2)]
        s_score = sem("s_score")
        s_exp = sem("s_exp")
        s_lo = sem("s_lo")
        s_lo_pool = sem("s_lo_pool")
        s_main = sem("s_main")
        s_acc = sem("s_acc")
        s_sq = sem("s_sq")
        s_av = sem("s_av")
        s_bg = sem("s_bg")
        s_dve = sem("s_dve")
        s_pool = sem("s_pool")
        s_act = sem("s_act")

        qs = Queues()
        put = qs.put

        def dve(fn, *waits):
            return put("dve", fn, waits, s_dve)

        def pool(fn, *waits):
            return put("pool", fn, waits, s_pool)

        def act(fn, *waits):
            return put("act", fn, waits, s_act)

        def dma(dst, src, s, *waits):
            return put("sp", partial(nc.sync.dma_start, dst, src), waits, s, 16)

        bg_banks = deque([spare, av0, *acc])

        def take():
            bg_banks.rotate(-1)
            return bg_banks[0]

        def bg_mm(bg, fns, *waits):
            for fn in fns[:-1]:
                put("pe", fn, (*waits, *bg.free))
            return put("pe", fns[-1], (*waits, *bg.free), s_bg)

        def bg_steps(bg, fns, *waits):
            for fn in fns[:-1]:
                put("pe", fn, (*waits, *bg.free))
                yield
            put("pe", fns[-1], (*waits, *bg.free), s_bg)

        def bg_read(bg, fn, *waits):
            t = dve(fn, *waits)
            bg.free = [t]
            return t

        state = {"ring_used": [None] * RING, "x1": [()] * B, "x_in": None, "ctx_t": None,
                 "w_q": None, "w": None, "part": 0, "vst": 0,
                 "part_out": [None, None], "v_out": [None, None],
                 "qk_done": [[()] * NM for _ in range(2 * B)], "v_done": [()] * 2 * B, "v_block": [None, None]}

        later = deque()
        now = [0]

        def settle():
            while later:
                later.popleft()[1]()

        def project(u):
            first = u == 0
            v_text, v_ip = (first_v_text, first_v_ip) if first else (w_text, w_ip)
            layer, b = units[u]
            tasks = []
            box = {}

            def loads():
                src = a["xT"][b] if layer == 0 else x1_scr[b]
                for m in range(NM):
                    box["x"] = dma(x_in[0:mw[m], m, :], src[P * m:P * m + mw[m], :], s_x,
                                   state["x_in"], *(state["x1"][b] if layer else ()))
                    box["wq"] = dma(w_q[0:mw[m], m, :], a[f"wq{layer}"][P * m:P * m + mw[m], :], s_wq,
                                    state["w_q"])
                dma(w_text[:, :, 0:D], a[f"wk{layer}"].rearrange("(c p) n -> p c n", p=P), s_w, state["w"])
                box["ctx"] = dma(ctx_t[:], a["ctxT"][b].rearrange("(c p) t -> p c t", p=P), s_ctx,
                                 state["ctx_t"])
                box["wk"] = dma(w_ip[:], a[f"wkip{layer}"].rearrange("(c p) n -> p c n", p=P), s_w, state["w"])
            tasks.append(loads)

            def split3(bg, m, n, dst):
                settle()
                w = mw[m]
                i = state["part"] % 2
                state["part"] += 1
                f, r, h = part_f[0:w, i, 0:n], part_r[0:w, i, 0:n], part_bf[0:w, i, :, 0:n]
                t = bg_read(bg, partial(nc.vector.tensor_copy, f, bg[0:w, 0:n]), (s_bg, s_bg.value), state["part_out"][i],
                            xout_free[i])
                t = dve(partial(nc.vector.tensor_copy, h[:, 0, :], f), t)
                t = pool(partial(nc.gpsimd.tensor_tensor, r, f, h[:, 0, :], ALU.subtract), t)

                def lower():
                    t1 = dve(partial(nc.vector.tensor_copy, h[:, 1, :], r), t)
                    t1 = pool(partial(nc.gpsimd.tensor_tensor, h[:, 2, :], r, h[:, 1, :], ALU.subtract), t1)
                    state["part_out"][i] = put("sp", partial(nc.sync.dma_start, dst, h),
                                               (t1,), s_part[i], 16)
                    state["qk_done"][u][m] = tuple(x for x in state["part_out"] if x)
                later.append((now[0] + 2, lower))

            def q_task(m):
                def go():
                    w, bg = mw[m], take()
                    yield from bg_steps(bg, [partial(nc.tensor.matmul, bg[0:w, 0:SQ], w_q[0:mw[k], k, P * m:P * m + w],
                                                   x_in[0:mw[k], k, :], start=(k == 0), stop=(k == NM - 1))
                           for k in range(NM)], box["x"], box["wq"])
                    state["x_in"] = state["w_q"] = (s_bg, s_bg.value)
                    split3(bg, m, SQ, q_scr[u, :, P * m:P * m + w, :].rearrange("j p t -> p j t"))
                return go

            def k_task(m, half):
                def go():
                    w, bg = mw[m], take()
                    t0 = half * 512
                    edge = (TEXT0 if layer == 0 else TEXT1) - t0
                    edge = max(0, min(512, edge))
                    fns = []
                    for wt, lo, hi in ((w_text, 0, edge), (w_ip, edge, 512)):
                        for k in range(NE):
                            if hi > lo:
                                fns.append(partial(nc.tensor.matmul, bg[0:w, lo:hi], wt[:, k, P * m:P * m + w], ctx_t[:, k, t0 + lo:t0 + hi],
                                    start=(k == 0), stop=(k == NE - 1)))
                    yield from bg_steps(bg, fns, box["ctx"], box["wk"])
                    state["w"] = state["ctx_t"] = (s_bg, s_bg.value)
                    split3(bg, m, 512, k_scr[u, :, P * m:P * m + w, t0:t0 + 512].rearrange("j p t -> p j t"))
                return go
            for m in range(NM):
                tasks.append((NM, q_task(m)))
                tasks += [(NE * (1 + (half == (0 if layer else 1))), k_task(m, half)) for half in range(T // 512)]

            def v_loads():
                free = None if first else state["w"]
                s = s_wv0 if first else s_w
                dma(v_text[:, :, 0:D], a[f"wv{layer}"].rearrange("(c p) n -> p c n", p=P), s, free)
                box["wv"] = dma(v_ip[:, :, :], a[f"wvip{layer}"].rearrange("(c p) n -> p c n", p=P), s, free)
            tasks.append(v_loads)

            ip_cols = ctx_t[:, :, T - IP:T]

            def ip_norm():
                t = dve(partial(nc.vector.tensor_tensor, ip_sq[:], ip_cols, ip_cols, ALU.mult), box["ctx"])
                bg = take()
                bg_mm(bg, [partial(nc.tensor.matmul, bg[:, 0:IP], ones[:], ip_sq[:, k, :],
                                               start=(k == 0), stop=(k == NE - 1)) for k in range(NE)], t, t_mem)
                t = bg_read(bg, partial(nc.vector.tensor_copy, ip_n[:, 0, :], bg[:, 0:IP]), (s_bg, s_bg.value))
                box["root"] = act(partial(nc.scalar.activation, ip_n[:, 1, :], ip_n[:, 0, :], ACT.Sqrt), t)

            def ip_scale():
                t = dve(partial(nc.vector.tensor_scalar, ip_n[:, 0, :], ip_n[:, 1, :], EPS, None, ALU.max), box["root"])
                t = dve(partial(nc.vector.reciprocal, ip_n[:, 1, :], ip_n[:, 0, :]), t)
                box["ipn"] = dve(partial(nc.vector.tensor_tensor, v_text[:, :, D:D + IP], ip_cols, ip_n[:, 1:2, :].broadcast_to([P, NE, IP]), ALU.mult),
                    t, state["w"])

            def ip_values():
                t = dve(partial(nc.vector.tensor_copy, ip_rep[:], ip_cols.rearrange("p c (o n) -> p c o n", o=1).broadcast_to([P, NE, HEADS, IP])),
                    box["ctx"])
                bg = take()
                bg_mm(bg, [partial(nc.tensor.matmul, bg[0:HEADS * IP, 0:D],
                                               ip_rep[:, k, :, :].rearrange("p h n -> p (h n)"), v_ip[:, k, :],
                                               start=(k == 0), stop=(k == NE - 1)) for k in range(NE)],
                      t, box["wv"])
                state["v_block"][b % 2] = bg_read(bg, partial(nc.vector.tensor_tensor, v_block[:, b % 2, :], bg[0:HEADS * IP, 0:D], head_block[:], ALU.mult),
                    (s_bg, s_bg.value), t_const)
                state["w"] = state["ctx_t"] = (s_bg, s_bg.value)
            if layer == 0:
                tasks += [ip_norm, ip_values, ip_scale]

            def v_task(blk):
                def go():
                    text = layer == 0 or blk == NT
                    c = 0 if blk == NT else blk
                    w = TEXT1 if blk == NT else P
                    n = D + IP if layer == 0 else D
                    bg = take()
                    wt = v_text if text else v_ip
                    yield from bg_steps(bg, [partial(nc.tensor.matmul, bg[0:w, 0:n], ctx_t[:, k, c * P:c * P + w], wt[:, k, 0:n],
                                                   start=(k == 0), stop=(k == NE - 1)) for k in range(NE)],
                          box["ctx"], box["wv"], box.get("ipn"))
                    state["w"] = state["ctx_t"] = (s_bg, s_bg.value)
                    i = state["vst"] % 2
                    state["vst"] += 1
                    f, st = v_f[0:w, i, :], v_stage[0:w, i, :, :]
                    vf = f[:, 0:D].rearrange("p (h d) -> p h d", d=DH)
                    stf = v_stage.bitcast(F32)[0:w, i, :, :]
                    free = state["v_out"][i]
                    one = ip_rows if layer == 1 and blk == 0 else ones_col
                    t = bg_read(bg, partial(nc.vector.tensor_scalar, f[:, 0:n], bg[0:w, 0:n], one[0:w, 0:1], None, ALU.mult),
                                (s_bg, s_bg.value), free, t_const, t_mem)
                    t1 = dve(partial(nc.vector.tensor_copy, st[:, :, 0:DH], vf), t)
                    t2 = dve(partial(nc.vector.tensor_copy, st[:, :, 2 * DH:2 * DH + 1], one[0:w, 0:1].rearrange("p (a b) -> p a b", a=1).broadcast_to([w, HEADS, 1])), free)
                    t3 = pool(partial(nc.gpsimd.tensor_tensor, st[:, :, DH:2 * DH], vf, stf[:, :, 0:DH], ALU.subtract), t1)
                    cols = 2 * DH + 1
                    if layer == 0:
                        ctx_ip = f[:, D:D + IP].rearrange("p (a n) -> p a n", a=1).broadcast_to([w, HEADS, IP])
                        t2 = dve(partial(nc.vector.tensor_copy, st[:, :, cols:cols + IP], ctx_ip), t)
                        t2 = dve(partial(nc.vector.tensor_tensor, st[:, :, cols + IP:cols + 2 * IP], ctx_ip,
                                                           stf[:, :, cols:cols + IP], ALU.subtract), t2)
                        cols += 2 * IP
                    state["v_out"][i] = put("sp", partial(nc.sync.dma_start, v_scr[u, blk, 0:w, :].rearrange("p (h v) -> p h v", v=VCOLS)[:, :, 0:cols], stf[:, :, 0:cols]),
                        (t2, t3), s_vout[i], 16)
                    state["v_done"][u] = tuple(x for x in state["v_out"] if x)
                return go
            tasks += [(NE, v_task(blk)) for blk in range(NT if layer == 0 else NT + 1)]
            return tasks

        def load_qk(g):
            u, gi = seq[g]
            layer, slot = units[u][0], g % RING
            h0 = gi * GROUP
            w = (state["ring_used"][slot], *state["qk_done"][u][h0 * DH // P])
            for j in range(GROUP):
                dma(k_ring[96:102, slot, j, :], row_scr[:, layer, :], s_ring[slot], t_row_const, *w)
            for i in range(6):
                rows = slice(DH * i, DH * i + DH)
                dma(k_ring[rows, slot, :, :],
                    k_scr[u, K_PARTS[i], h0 * DH:(h0 + GROUP) * DH, :].rearrange("(h d) t -> d h t", d=DH),
                    s_ring[slot], *w)
                t = dma(q_ring[rows, slot, :, :],
                        q_scr[u, Q_PARTS[i], h0 * DH:(h0 + GROUP) * DH, :].rearrange("(h d) t -> d h t", d=DH),
                        s_ring[slot], *w)
            ring_ready[g] = t

        def load_v(g):
            u, gi = seq[g]
            layer, slot = units[u][0], g % RING
            h0 = gi * GROUP
            w = (state["ring_used"][slot], *state["v_done"][u])
            cols = slice(h0 * VCOLS, (h0 + GROUP) * VCOLS)
            if layer == 0:
                t = dma(v_ring.bitcast(F32)[:, slot, 0:NT, :], v_scr[u, 0:NT, :, cols].rearrange("b p v -> p b v"),
                        s_ring_v[slot], *w)
            else:
                for j in range(GROUP):
                    c0 = (h0 + j) * VCOLS
                    dma(v_ring.bitcast(F32)[:, slot, 0:NT, j * VCOLS:j * VCOLS + 33],
                        v_scr[u, 0:NT, :, c0:c0 + 33].rearrange("b p v -> p b v"), s_ring_v[slot], *w)
                    t = dma(v_ring.bitcast(F32)[0:TEXT1, slot, NT, j * VCOLS:j * VCOLS + 33],
                            v_scr[u, NT, 0:TEXT1, c0:c0 + 33], s_ring_v[slot], *w)
            v_ready[g] = t

        v_ready = {}
        ring_ready = {}
        rows_ready = {}

        def maxima(g):
            u, gi = seq[g]
            layer, slot, gp = units[u][0], g % RING, g % 2
            tasks = []
            last = {}

            def half_task(j, st, half):
                def go():
                    bg = take()
                    bg_mm(bg, [partial(nc.tensor.matmul, bg[:, :], q_ring[0:96, slot, j, st * P:(st + 1) * P],
                                              k_ring[0:96, slot, j, half * 512:(half + 1) * 512],
                                              start=True, stop=True)], ring_ready[g])
                    ready = (s_bg, s_bg.value)
                    mp = max_parts[:, gp, j, st, :]

                    def top(i, lo, hi):
                        return bg_read(bg, partial(nc.vector.tensor_reduce, mp[:, i:i + 1], bg[:, lo:hi], AX_X, ALU.max), ready)
                    if layer == 0:
                        top(half, 0, 512 if half == 0 else 512 - IP)
                        if half == 1:
                            bg_read(bg, partial(nc.vector.tensor_copy, ip_scores[:, u % 2, st, gi * GROUP + j, :],
                                                            bg[:, 512 - IP:512]), ready)
                    elif half == 0:
                        top(0, 0, TEXT1)
                        top(1, TEXT1, 512)
                    else:
                        top(2, 0, 512)
                    last["t"] = bg.free[0]
                return go
            tasks += [half_task(j, st, half) for j in range(GROUP) for st in range(ST) for half in range(2)]

            def rows_task():
                mp = max_parts[:, gp, :, :, :].rearrange("p j s k -> p (j s) k")
                if layer == 0:
                    t = dve(partial(nc.vector.tensor_reduce, neg_max[:, gp, 0, :], mp[:, :, 0:2], AX_X, ALU.max,
                                                      negate=True), last["t"])
                else:
                    dve(partial(nc.vector.tensor_scalar, neg_max[:, gp, 0, :], mp[:, :, 0], -1.0, None, ALU.mult), last["t"])
                    t = dve(partial(nc.vector.tensor_reduce, neg_max[:, gp, 1, :], mp[:, :, 1:3], AX_X, ALU.max,
                                                      negate=True), last["t"])
                n, bg = MR * (layer + 1), take()
                bg_mm(bg, [partial(nc.tensor.transpose, bg[0:n, 0:P], neg_max[:, gp, 0:layer + 1, :].rearrange("p a b -> p (a b)"),
                                             ident[:])], t, t_const)
                bf = max_bf[0:n, gp, :, :]
                t = bg_read(bg, partial(nc.vector.tensor_copy, max_t[0:n, :], bg[0:n, 0:P]), (s_bg, s_bg.value),
                            rows_ready.get(g - 2))
                t = dve(partial(nc.vector.tensor_copy, bf[:, 0, :], max_t[0:n, :]), t)
                t = dve(partial(nc.vector.tensor_tensor, max_r[0:n, :], max_t[0:n, :], bf[:, 0, :], ALU.subtract), t)
                t = dve(partial(nc.vector.tensor_copy, bf[:, 1, :], max_r[0:n, :]), t)
                t = dve(partial(nc.vector.tensor_tensor, bf[:, 2, :], max_r[0:n, :], bf[:, 1, :], ALU.subtract), t)
                for k in range(layer + 1):
                    for i in range(3):
                        row = 96 + 3 * k + i
                        r = dma(q_ring[row:row + 1, slot, :, :].rearrange("p j (s c) -> p (j s) c", c=P),
                                max_bf[MR * k:MR * k + MR, gp, i, :], s_rows[slot], t, ring_ready[g])
                rows_ready[g] = r
            tasks.append(rows_task)
            return tasks

        tok_ready = {}
        tok_free = [None] * NT
        tok_split = [None, None]
        tok_here = {}

        def fetch_tokens(b, c):
            i = c % 2
            tok_here[c] = put("sp", partial(nc.sync.dma_start, tok_stage[:, i, :], a["ctx"][b, c * P:(c + 1) * P, :]),
                              (tok_split[i],), s_tok[i], 16)

        def split_tokens(b, c):
            i = c % 2
            t1 = dve(partial(nc.vector.tensor_copy, tok_hi[:, c, :], tok_stage[:, i, :]), tok_here[c], tok_free[c])
            t2 = pool(partial(nc.gpsimd.tensor_tensor, tok_lo[:, c, :], tok_stage[:, i, :],
                                                tok_hi.bitcast(F32)[:, c, :], ALU.subtract), t1)
            tok_split[i] = t2
            tok_ready[(b, c)] = t2

        heads_read = [None, None]

        def bc(v, n):
            return v.rearrange("p (x o) -> p x o", o=1).broadcast_to([P, HS, n])

        def close(u):
            layer, b = units[u]
            par = b % 2
            tasks = []
            box = {}
            ho = heads_out[layer][:, :, :, :].rearrange("p s h v -> p (s h) v")
            at = attn[:].rearrange("p s h d -> p (s h) d")
            rs, rs2 = small[:, layer, :], small[:, 2, :]
            fu = fused.rearrange("p (x n) -> p x n", n=IP)
            w4v = w4.rearrange("p (x n) -> p x n", n=IP)

            def combine():
                done = (s_dve, s_dve.value)
                t1 = dve(partial(nc.vector.reciprocal, rs, ho[:, :, SUM_COL[layer]]), done)
                if layer == 0:
                    dve(partial(nc.vector.tensor_copy, w4v, ho[:, :, CTX_COL:CTX_COL + IP]), done)
                    box["rs"] = t1
                    box["attn"] = heads_read[0] = dve(partial(
                        nc.vector.tensor_tensor, at, ho[:, :, 0:DH], bc(rs, DH), ALU.mult), t1)
                else:
                    t2 = dve(partial(nc.vector.reciprocal, rs2, ho[:, :, SUM_COL[1] + 1]), done)
                    t = dve(partial(nc.vector.tensor_tensor, at, ho[:, :, 0:DH], bc(rs, DH), ALU.mult), t1)
                    image = ho[:, :, DH:2 * DH]
                    t2 = dve(partial(nc.vector.tensor_tensor, image, image, bc(rs2, DH), ALU.mult), t2)
                    box["attn"] = heads_read[1] = dve(partial(nc.vector.tensor_tensor, at, at, image, ALU.add), t, t2)
            tasks.append(combine)

            def fuse():
                nrm, n2 = small[:, 3, :], small[:, 4, :]
                t = act(partial(nc.scalar.activation, nrm, sum_sq[:, par, :, :].rearrange("p s h -> p (s h)"), ACT.Sqrt),
                        (s_sq, s_sq.value))
                box["nrm"] = t

            def fuse_exp():
                nrm, n2 = small[:, 3, :], small[:, 4, :]
                t = dve(partial(nc.vector.tensor_tensor, nrm, nrm, rs, ALU.mult), box["nrm"], box["rs"])
                t = dve(partial(nc.vector.tensor_scalar, nrm, nrm, EPS, None, ALU.max), t)
                t = dve(partial(nc.vector.reciprocal, n2, nrm), t)
                t = dve(partial(nc.vector.tensor_tensor, n2, n2, rs, ALU.mult), t)
                t = dve(partial(nc.vector.tensor_tensor, w4v, w4v, bc(n2, IP), ALU.mult), t)
                t = dve(partial(nc.vector.tensor_scalar, w4v, w4v, SEM_SCALE, None, ALU.mult), t)
                t = dve(partial(nc.vector.scalar_tensor_tensor, fu, ip_scores[:, par, :, :, :].rearrange("p s h n -> p (s h) n"), SCALE, w4v,
                    ALU.mult, ALU.add), t, state["ctx_t"])
                t = dve(partial(nc.vector.tensor_reduce, nrm, fu, AX_X, ALU.max), t)
                t = dve(partial(nc.vector.tensor_tensor, fu, fu, bc(nrm, IP), ALU.subtract), t)
                box["exp"] = act(partial(nc.scalar.activation, fused, fused, ACT.Exp), t)

            def fuse_probs():
                nrm, n2 = small[:, 3, :], small[:, 4, :]
                t = box["exp"]
                t = dve(partial(nc.vector.tensor_reduce, nrm, fu, AX_X, ALU.add), t)
                t = dve(partial(nc.vector.reciprocal, n2, nrm), t)
                n2s = n2.rearrange("p (s h) -> p s h", h=HEADS)
                t = dve(partial(nc.vector.tensor_tensor, n2s, n2s, mask_s[:].rearrange("p (s o) -> p s o", o=1).broadcast_to([P, ST, HEADS]), ALU.mult),
                    t, t_const)
                box["probs"] = dve(partial(nc.vector.tensor_tensor, fu, fu, bc(n2, IP), ALU.mult), t)

            def probs_rows():
                bg = take()
                bg_mm(bg, [partial(nc.tensor.transpose, bg[0:HEADS * IP, st * P:(st + 1) * P],
                                                    fused[:, st * HEADS * IP:(st + 1) * HEADS * IP], ident[:])
                       for st in range(ST)], box["probs"], t_const)
                box["pt"] = bg_read(bg, partial(nc.vector.tensor_copy, probs_t, bg[0:HEADS * IP, :]), (s_bg, s_bg.value), state["ctx_t"])
            if layer == 0:
                tasks += [fuse, fuse_exp, fuse_probs, probs_rows]

            def turn(m):
                def go():
                    w, bg = mw[m], take()
                    fl = [attn[:, st, :, :].rearrange("p h d -> p (h d)")[:, P * m:P * m + w] for st in range(ST)]
                    if layer == 0:
                        fns = [partial(nc.tensor.matmul, bg[0:w, :], v_block[:, par, P * m:P * m + w], probs_t,
                                                  start=True, stop=True)]
                        fns += [partial(nc.tensor.matmul, bg[0:w, st * P:(st + 1) * P], fl[st], ident[:],
                                                          start=False, stop=True, skip_group_check=True)
                                for st in range(ST)]
                        yield from bg_steps(bg, fns, box["attn"], box["pt"], state["v_block"][par], t_const)
                    else:
                        bg_mm(bg, [partial(nc.tensor.transpose, bg[0:w, st * P:(st + 1) * P], fl[st], ident[:])
                               for st in range(ST)], box["attn"], t_const)
                    box["o"] = bg_read(bg, partial(nc.vector.tensor_copy, o_t[0:w, m, :], bg[0:w, :]), (s_bg, s_bg.value), state["ctx_t"])
                return go

            res = {}

            def load_residual(m):
                w, i = mw[m], m % 2
                src = a["xT"][b] if layer == 0 else x1_scr[b]
                settle()
                res[m] = put("sp", partial(nc.sync.dma_start, x_res[0:w, i, :], src[P * m:P * m + w, :]),
                             (fin_free[i], state["part_out"][i], *(state["x1"][b] if layer else ())), s_res[i], 16)

            tasks += [partial(load_residual, 0), partial(load_residual, 1)]
            tasks += [(ST + 1 if layer == 0 else 1, turn(m)) for m in range(NM)]

            def finish(m):
                def go():
                    w, i, bg = mw[m], m % 2, take()
                    yield from bg_steps(bg, [partial(nc.tensor.matmul, bg[0:w, :], w_o[layer][0:mw[k], k, P * m:P * m + w],
                                                   o_t[0:mw[k], k, :], start=(k == 0), stop=(k == NM - 1))
                           for k in range(NM)], box["o"], *t_wo)
                    state["ctx_t"] = (s_bg, s_bg.value)
                    t = bg_read(bg, partial(nc.vector.scalar_tensor_tensor, x_out[0:w, i, :], bg[0:w, :], bias[0:w, layer, m:m + 1], x_res[0:w, i, :],
                        ALU.add, ALU.add), (s_bg, s_bg.value), res[m], xout_free[i])
                    fin_free[i] = t
                    dst = (x1_scr if layer == 0 else out)[b, P * m:P * m + w, :]
                    xout_free[i] = put("sp", partial(nc.sync.dma_start, dst, x_out[0:w, i, :]), (t,), s_xout[i], 16)
                    if layer == 0:
                        state["x1"][b] = tuple(xout_free)
                    if m + 2 < NM:
                        load_residual(m + 2)
                return go
            tasks += [(NM, finish(m)) for m in range(NM)]
            return tasks

        t_wo = []

        def load_w_o():
            for layer in range(2):
                for m in range(NM):
                    dma(w_o[layer][0:mw[m], m, :], a[f"wo{layer}"][P * m:P * m + mw[m], :], s_wo)
                    t_wo[:] = [dma(bias[0:mw[m], layer, m:m + 1], a[f"b{layer}"][P * m:P * m + mw[m], :], s_wo)]

        fin_free, xout_free = [None, None], [None, None]

        chunks = [(g, u, gi * GROUP + j, c) for g, (u, gi) in enumerate(seq) for j in range(GROUP) for c in range(NT)]
        exp_done = {}
        lo_done = {}
        main_done = {}
        rows_free = [None, None]

        def rows_of(u, c):
            return P - IP if units[u][0] == 0 and c == NT - 1 else P

        def scores(n):
            g, u, h, c = chunks[n]
            layer = units[u][0]
            j = h % GROUP
            slot, kk = g % RING, rows_of(u, c)
            depth = 96 + 3 * (layer + 1)
            bank_s, ps, es = score[n % 2], n % P_SLOTS, n % E_SLOTS
            t = put("pe", partial(nc.tensor.matmul, bank_s[0:kk, :], k_ring[0:depth, slot, j, c * P:c * P + kk],
                                             q_ring[0:depth, slot, j, :], start=True, stop=True),
                    (ring_ready[g], rows_ready[g], exp_done.get(n - 2)), s_score)
            put("act", partial(nc.scalar.activation, prob[0:kk, es, :], bank_s[0:kk, :], ACT.Exp, scale=SCALE),
                (t, lo_done.get(n - E_SLOTS)))
            exp_done[n] = put("act", partial(nc.scalar.activation, prob_hi[0:kk, ps, :], bank_s[0:kk, :], ACT.Exp,
                                                            scale=SCALE),
                              (t, main_done.get(n - P_SLOTS)), s_exp)

        def low_part(n):
            g, u, h, c = chunks[n]
            kk, ps, es = rows_of(u, c), n % P_SLOTS, n % E_SLOTS
            on_pool = units[u][0] == 1 and n % 8 in POOL_LOW
            unit = nc.gpsimd if on_pool else nc.vector
            lo_done[n] = put("pool" if on_pool else "dve", partial(unit.tensor_tensor,
                prob_lo[0:kk, ps, :], prob[0:kk, es, :], prob_hi.bitcast(F32)[0:kk, ps, :], ALU.subtract),
                (exp_done[n], main_done.get(n - P_SLOTS)), s_lo_pool if on_pool else s_lo)

        def products0(n, slot_hook):
            g, u, h, c = chunks[n]
            j = h % GROUP
            slot, kk, ps = g % RING, rows_of(u, c), n % P_SLOTS
            b = units[u][1]
            first, last = c == 0, c == NT - 1
            for turn_no, st in enumerate((3, 1, 0, 2)):
                cols = slice(st * P, (st + 1) * P)
                w = [exp_done[n], tok_ready[(b, c)]] + (acc[st].free if first else [])
                put("pe", partial(nc.tensor.matmul, acc[st][:, :], prob_hi[0:kk, ps, cols], tok_hi[0:kk, c, :],
                                             start=first, stop=False), w)
                put("pe", partial(nc.tensor.matmul, acc[st][:, :], prob_hi[0:kk, ps, cols], tok_lo[0:kk, c, :],
                                             start=False, stop=False))
                t = put("pe", partial(nc.tensor.matmul, acc[st][:, :], prob_lo[0:kk, ps, cols], tok_hi[0:kk, c, :],
                                                 start=False, stop=last), (lo_done[n],),
                        s_acc if last else None)
                if last:
                    ts = put("act", partial(nc.scalar.activation, squares[:, turn_no % 2, :], acc[st][:, :], ACT.Square,
                        accum_out=sum_sq[:, u % 2, st, h:h + 1]), (t, (s_sq, s_sq.value - 1)), s_sq)
                    acc[st].free = [ts]
                slot_hook()
            for i, pr in enumerate((prob_hi, prob_lo)):
                t = put("pe", partial(nc.tensor.matmul, av0[0:VCOLS, :], v_ring[0:kk, slot, c, j * VCOLS:(j + 1) * VCOLS], pr[0:kk, ps, :],
                    start=(first and i == 0), stop=(last and i == 1)), (*av0.free, v_ready[g]),
                    s_main if i else None)
            main_done[n] = t
            tok_free[c] = t
            if last:
                r = 64 * j
                t = put("act", partial(nc.scalar.activation, out_rows[r:r + VCOLS, 1, :], av0[0:VCOLS, :], ACT.Copy),
                        (t, rows_free[1], t_mem), s_av)
                av0.free = [t]
                if j == GROUP - 1:
                    urgent.append((n + 1, lambda: turn_head(u, h, t)))
                if h == HEADS - 1:
                    urgent.append((n + 1, lambda: unit_done(u)))

        evac = deque()

        def products1(n):
            g, u, h, c = chunks[n]
            j = h % GROUP
            slot, ps = g % RING, n % P_SLOTS
            first, last = c == 0, c == NT - 1
            image, text = acc[2 * (h % 2)], acc[1]
            M = 2 * DH + 1
            vc = slice(j * VCOLS, j * VCOLS + M)
            for i, pr in enumerate((prob_hi, prob_lo)):
                w = [v_ready[g], exp_done[n] if i == 0 else lo_done[n]]
                if first:
                    w += [*image.free, *text.free]
                    put("pe", partial(nc.tensor.matmul, text[0:M, :], v_ring[0:TEXT1, slot, NT, vc],
                                           pr[0:TEXT1, ps, :], start=(i == 0), stop=(i == 1)), w)
                t = put("pe", partial(nc.tensor.matmul, image[0:M, :], v_ring[:, slot, c, vc], pr[:, ps, :],
                                      start=(first and i == 0), stop=(last and i == 1)), w, s_main if i else None)
            main_done[n] = t
            evac.append((n, first, last))

        def evacuate(n):
            if not evac or evac[0][0] != n:
                return
            _, first, last = evac.popleft()
            g, u, h, c = chunks[n]
            image, text, M = acc[2 * (h % 2)], acc[1], 2 * DH + 1
            if first:
                text.free = [put("act", partial(nc.scalar.activation, out_rows[0:M, h % 2, :], text[0:M, :], ACT.Copy),
                                 (main_done[n], rows_free[h % 2], t_mem), s_av)]
            if last:
                tb = put("act", partial(nc.scalar.activation, out_rows[64:64 + M, h % 2, :], image[0:M, :], ACT.Copy),
                         (main_done[n], rows_free[h % 2]), s_av)
                image.free = [tb]
                urgent.append((n + 3, lambda: turn_head(u, h, tb)))
                if h == HEADS - 1:
                    urgent.append((n + 3, lambda: unit_done(u)))

        def turn_head(u, h, t):
            layer = units[u][0]
            w = 64 + (VCOLS if layer == 0 else 2 * DH + 1)
            side = 1 if layer == 0 else h % 2
            bg = take()
            bg_mm(bg, [partial(nc.tensor.transpose, bg[:, st * P:st * P + w], out_rows[0:w, side, st * P:(st + 1) * P],
                                                ident[0:w, 0:w]) for st in range(ST)], t, t_const)
            rows_free[side] = (s_bg, s_bg.value)
            src = bg[:, :].rearrange("p (s v) -> p s v", v=P)
            ready = (s_bg, s_bg.value)

            def add_parts(head, dst, lo, n):
                bg_read(bg, partial(nc.vector.tensor_reduce, heads_out[layer][:, :, head, dst:dst + n],
                                    src[:, :, lo:lo + 2 * n].rearrange("p s (k d) -> p s d k", k=2),
                                    AX_X, ALU.add), ready, heads_read[layer])
            if layer == 0:
                for j in range(GROUP):
                    head, r = h - GROUP + 1 + j, 64 * j
                    add_parts(head, 0, r, DH)
                    add_parts(head, CTX_COL, r + 2 * DH + 1, IP)
                bg_read(bg, partial(nc.vector.tensor_copy, heads_out[0][:, :, h - 1:h + 1, SUM_COL[0]],
                                    src[:, :, 2 * DH:2 * DH + 65:64]), ready, heads_read[0])
            else:
                add_parts(h, 0, 0, DH)
                add_parts(h, DH, 64, DH)
                bg_read(bg, partial(nc.vector.tensor_copy, heads_out[1][:, :, h, SUM_COL[1]:SUM_COL[1] + 2],
                                    src[:, :, 2 * DH:2 * DH + 65:64]), ready, heads_read[1])

        urgent = deque()
        bgq = deque()
        current = []

        def run_step():
            if current:
                if next(current[0], "end") == "end":
                    current.clear()
                return
            if urgent and urgent[0][0] <= now[0]:
                task = urgent.popleft()[1]
            elif bgq:
                task = bgq.popleft()
                task = task[1] if isinstance(task, tuple) else task
            else:
                return
            run = task()
            if run is not None:
                current.append(run)
                run_step()

        def run_all(*tasks):
            bgq.extend(tasks)
            while bgq or current:
                run_step()

        def steps_of(tasks):
            return sum(t[0] if isinstance(t, tuple) else 1 for t in tasks)

        first_unit = project(0)
        n_qk = 3 * NM
        first_loads, first_qk, first_v_loads, *first_v = (
            first_unit[0], first_unit[1:1 + n_qk], *first_unit[1 + n_qk:])
        t = dma(row_const_f, a["row_const"], s_rowf)
        t = dve(partial(nc.vector.tensor_copy, k_ring[0:6, RING - 1, :, :], row_const_f), t)
        first_loads()
        t_row_const = dma(row_scr[:, :, :], k_ring[0:6, RING - 1, :, :], s_rowc, t)
        first_v_loads()
        t_const = [dma(ident[:], a["ident"], s_const), dma(head_block[:], a["head_block"], s_const),
                   dma(ip_rows[:], a["ip_rows"], s_const), dma(mask_s[:], a["mask"], s_const)][-1]
        put("dve", partial(nc.vector.memset, ones[:], 1.0), (), s_mem)
        put("dve", partial(nc.vector.memset, ones_col[:], 1.0), (), s_mem)
        t_mem = put("dve", partial(nc.vector.memset, out_rows[:], 0.0), (), s_mem)

        run_all(*first_qk[0:6])
        settle()
        load_qk(0)
        for c in range(2):
            fetch_tokens(0, c)
        run_all(*first_v[0:5])
        rest, top = first_v[5:], maxima(0)
        while rest or top:
            run_all(*rest[:1], *top[:2])
            rest, top = rest[1:], top[2:]
        heads_read[0] = (s_bg, s_bg.value)
        settle()
        load_v(0)
        for c in range(2):
            split_tokens(0, c)
        load_qk(1)
        for c in range(2, 4):
            fetch_tokens(0, c)
            split_tokens(0, c)
        groups = len(seq)

        jobs = []

        def add_job(tasks, deadline):
            jobs.append([deadline, deque(tasks)])

        def unit_done(u):
            layer, b = units[u]
            combine, *rest = close(u)
            combine()
            if layer == 0:
                add_job(rest + project(B + b), place[(B + b, 0)] - LOOK_LOAD)
                if b + 2 < B:
                    add_job(project(u + 2), place[(u + 2, 0)] - LOOK_LOAD)
            else:
                add_job(rest, place[(b + 2, NG - 1)] if b + 2 < B else groups)

        def job_tasks(g):
            weight = [WEIGHT[units[u][0]] for u, _ in seq]
            total, rate = 0, 0
            for d, tasks in sorted(jobs, key=lambda x: x[0]):
                total += steps_of(tasks)
                rate = max(rate, total / sum(weight[g:max(d, g + 1)]))
            quota = math.ceil(rate * weight[g])
            out = []
            while jobs and (quota > 0 or min(jobs, key=lambda x: x[0])[0] <= g):
                if under_way and under_way[0] in jobs:
                    job = under_way[0]
                else:
                    job = min(jobs, key=lambda x: x[0])
                    under_way[:] = [job]
                t = job[1].popleft()
                out.append(t)
                quota -= steps_of([t])
                if not job[1]:
                    jobs.remove(job)
                    under_way.clear()
            return out

        under_way = []
        slot_no, rest_until = [0], [0]
        add_job(first_qk[6:], place[(0, 2 * P // (GROUP * DH))] - LOOK_LOAD)
        add_job(project(1), place[(1, 0)] - LOOK_LOAD)
        top_tasks = deque(maxima(1))
        per_group = GROUP * NT
        now[0] = 0
        for n in range(AHEAD):
            scores(n)
            if n >= LOW_LAG:
                low_part(n - LOW_LAG)
        for g, (u, gi) in enumerate(seq):
            layer, b = units[u]
            bg_banks.clear()
            bg_banks.extend([spare] if layer == 0 else [spare, av0, acc[3]])
            mine = job_tasks(g)
            if g + LOOK_MAX < groups:
                top_tasks.extend(maxima(g + LOOK_MAX))
            keep = 0
            if layer == 1 and g + 1 < groups and units[seq[g + 1][0]][0] == 0:
                keep = len(top_tasks) // 4
            work = [top_tasks.popleft() for _ in range(len(top_tasks) - keep)]
            for i in range(max(len(work), 1)):
                bgq.extend(work[i:i + 1])
                n = max(len(work), 1)
                bgq.extend(mine[len(mine) * i // n:len(mine) * (i + 1) // n])
            slots = per_group * ST - 4 if layer == 0 else per_group
            total, done = steps_of(bgq), [0, 0]

            def hook():
                done[0] += 1
                while later and later[0][0] <= now[0]:
                    later.popleft()[1]()
                slot_no[0] += 1
                due = urgent and urgent[0][0] <= now[0]
                while due or ((bgq or current) and done[1] < -(-total * done[0] // slots)):
                    if layer == 0 and not current and slot_no[0] < rest_until[0]:
                        return
                    if not current and due:
                        due = False
                    else:
                        done[1] += 1
                    run_step()
                    if not current:
                        rest_until[0] = slot_no[0] + SPACING

            for n in range(g * per_group, (g + 1) * per_group):
                now[0] = n
                if n + AHEAD < len(chunks):
                    scores(n + AHEAD)
                if n + AHEAD - LOW_LAG < len(chunks):
                    low_part(n + AHEAD - LOW_LAG)
                evacuate(n - 1)
                if layer == 0:
                    products0(n, hook)
                else:
                    products1(n)
                    hook()
                _, _, h, c = chunks[n]
                if n < NT - 4:
                    fetch_tokens(0, n + 4)
                    if n == 0:
                        load_v(1)
                elif n == NT - 4:
                    for later_g in range(2, LOOK_LOAD + 1):
                        load_qk(later_g)
                        load_v(later_g)
                    load_w_o()
                if 1 <= n <= NT - 4:
                    split_tokens(0, n + 3)
                if layer == 0 and b + 1 < B:
                    if h == HEADS - 2 and c >= NT - 2:
                        fetch_tokens(b + 1, c - NT + 2)
                    elif h == HEADS - 1:
                        split_tokens(b + 1, c)
                        if c + 2 < NT:
                            fetch_tokens(b + 1, c + 2)
            run_all()
            state["ring_used"][g % RING] = main_done[(g + 1) * per_group - 1]
            if g + 1 + LOOK_LOAD < groups:
                settle()
                load_qk(g + 1 + LOOK_LOAD)
                load_v(g + 1 + LOOK_LOAD)
        evacuate(len(chunks) - 1)
        now[0] += 4
        while urgent:
            run_step()
        now[0] += 1
        run_all(*[t for job in jobs for t in job[1]])
        settle()
        qs.q["sp"].append(([x for x in xout_free], None, None, 0))

        block = ctx.enter_context(nc.Block())

        @block.tensor
        def _(e):
            qs.play("pe", e)

        @block.scalar
        def _(e):
            qs.play("act", e)

        @block.vector
        def _(e):
            qs.play("dve", e)

        @block.gpsimd
        def _(e):
            qs.play("pool", e)

        @block.sync
        def _(e):
            final = qs.q["sp"].pop()
            qs.play("sp", e)
            for s, v in final[0]:
                e.wait_ge(s.handle, v)
            for s in (*s_part, *s_vout, *s_xout):
                e.wait_ge(s.handle, s.value)


def kernel(**inputs):
    import numpy as np
    import concourse.bacc as bacc
    from concourse.bass_utils import run_bass_kernel_spmd

    f = {k: np.asarray(v) for k, v in inputs.items()}
    x, c = f["x"], f["ctx_2048"]
    B, S, D = x.shape
    T = c.shape[1]
    tr = lambda v: np.ascontiguousarray(np.swapaxes(v, -1, -2))
    row_const = np.zeros((6, 2, T), np.float32)
    row_const[:, 0, :] = 1.0
    row_const[0:3, 1, :TEXT1] = 1.0
    row_const[3:6, 1, TEXT1:] = 1.0
    ip_rows = np.ones((P, 1), np.float32)
    ip_rows[:TEXT1] = 0.0
    arrays = {
        "xT": tr(x), "ctxT": tr(c), "ctx": np.ascontiguousarray(c),
        "mask": tr(f["fside_S_0"].reshape(S // P, P)),
        "ident": np.eye(P, dtype=np.float32), "row_const": row_const, "ip_rows": ip_rows,
        "head_block": np.kron(np.eye(HEADS, dtype=np.float32), np.ones((IP, D // HEADS), np.float32)),
    }
    for name, key in (("wq", "W_q"), ("wk", "W_k"), ("wv", "W_v"), ("wkip", "W_k_ip"), ("wvip", "W_v_ip"),
                      ("wo", "W_out")):
        arrays[name + "0"] = np.ascontiguousarray(f["L0_xattn_" + key])
    for name, key in (("wq", "Wq"), ("wk", "Wk"), ("wv", "Wv"), ("wkip", "Wk_ip"), ("wvip", "Wv_ip"), ("wo", "Wo")):
        arrays[name + "1"] = tr(f["L1_xattn_" + key])
    arrays["b0"] = f["L0_xattn_b_out"].reshape(D, 1)
    arrays["b1"] = f["L1_xattn_bo"].reshape(D, 1)

    nc = bacc.Bacc("TRN2", target_bir_lowering=False, num_devices=1)
    aps = {k: nc.dram_tensor(f"in_{k}", v.shape, F32, kind="ExternalInput").ap() for k, v in arrays.items()}
    out = nc.dram_tensor("out_T", (B, D, S), F32, kind="ExternalOutput").ap()
    cross_attention_pair(nc, aps, out)
    r = run_bass_kernel_spmd(nc, [{f"in_{k}": v for k, v in arrays.items()}], core_ids=[0])
    return tr(r.results[0]["out_T"])
```
